# Optimizing a Trainium2 kernel written in Bass

```python
import numpy as np
import jax
import jax.numpy as jnp

def _softmax(x, axis=-1):
    return jax.nn.softmax(x, axis=axis)

def _gelu(x):
    return jax.nn.gelu(x, approximate=True)

def _silu(x):
    return jax.nn.silu(x)

def _sigmoid(x):
    return jax.nn.sigmoid(x)

def _layernorm(x, axis=-1, eps=1e-05):
    m = jnp.mean(x, axis=axis, keepdims=True)
    v = jnp.var(x, axis=axis, keepdims=True)
    return (x - m) / jnp.sqrt(v + eps)

def _scatter_add(tgt, idx, src, axis=0):
    return tgt.at[idx].add(src)

def _segment_sum(src, seg, n):
    return jax.ops.segment_sum(src, seg, n)
kernel_name = 'mk_decoder_preln_d1_seqx_r8_3325a3'

def setup_inputs(seed: int=0):
    np.random.seed(seed)
    _w = jnp.asarray

    def _rec_inputs():
        import jax
        import jax.numpy as jnp
        _rk = jax.random.key(seed)
        x = 0.5 + 0.2887 * jax.random.normal(jax.random.fold_in(_rk, 1), (4, 256, 256), jnp.float32)
        _lenS = 256 - jax.random.randint(jax.random.fold_in(_rk, 7), (4,), 0, max(1, 256 // 4) + 1, jnp.int32)
        _lenS2 = 256 - jax.random.randint(jax.random.fold_in(_rk, 8), (4,), 0, max(1, 256 // 4) + 1, jnp.int32)
        _ctx_512P = jax.random.normal(jax.random.fold_in(_rk, 11), (4, 16, 64), jnp.float32)
        _ctx_512c = jax.random.dirichlet(jax.random.fold_in(_rk, 511), 0.3 * jnp.ones((16,), jnp.float32), (4, 256))
        _ctx_512t = jnp.einsum('bsk,bkd->bsd', _ctx_512c, _ctx_512P)
        _ctx_512t = _ctx_512t * jax.lax.rsqrt(jnp.mean(jnp.square(_ctx_512t)) + 1e-12) * 0.953939
        ctx_512 = 7.22013e-05 + 1.00017 * (_ctx_512t + 0.3 * jax.random.normal(jax.random.fold_in(_rk, 611), (4, 256, 64), jnp.float32))
        _validS = jnp.arange(256)[None, :] < _lenS[:, None]
        _validS2 = jnp.arange(256)[None, :] < _lenS2[:, None]
        _causal = jnp.tril(jnp.ones((256, 256), dtype=bool))
        mask_SxS2_bk1 = jnp.broadcast_to(_validS2[0:1, :], (256, 256))
        mask_BxS2_bf0 = jnp.logical_not(jnp.ones((4, 256), dtype=bool))
        return (x, ctx_512, mask_SxS2_bk1, mask_BxS2_bf0)
    x, ctx_512, mask_SxS2_bk1, mask_BxS2_bf0 = _rec_inputs()

    def _L0_attn_setup():
        import jax, jax.numpy as jnp
        import numpy as np
        HID = 256
        HEADS = 16
        HD = HID // HEADS
        EPS = 1e-06

        def _heads(x, b, s):
            return x.reshape(b, s, HEADS, HD).transpose(0, 2, 1, 3)
        key = jax.random.key(seed)
        ks = jax.random.split(key, 9)
        s = 1.0 / np.sqrt(HID)
        return {'hidden_states': jax.random.normal(ks[0], (4, 512, HID), jnp.float32), 'q_w': jax.random.normal(ks[1], (HID, HID), jnp.float32) * s, 'q_b': jnp.zeros((HID,), jnp.float32), 'k_w': jax.random.normal(ks[2], (HID, HID), jnp.float32) * s, 'k_b': jnp.zeros((HID,), jnp.float32), 'v_w': jax.random.normal(ks[3], (HID, HID), jnp.float32) * s, 'v_b': jnp.zeros((HID,), jnp.float32), 'o_w': jax.random.normal(ks[4], (HID, HID), jnp.float32) * s, 'o_b': jnp.zeros((HID,), jnp.float32)}
    _L0_attn_all = _L0_attn_setup()
    _L0_attn_in = {k: v for k, v in _L0_attn_all.items() if k in ('q_w', 'q_b', 'k_w', 'k_b', 'v_w', 'v_b', 'o_w', 'o_b')}
    del _L0_attn_all

    def _L0_xattn_setup():
        import jax, jax.numpy as jnp
        import numpy as np
        B, S, H = (8, 256, 64)
        key = jax.random.key(seed)
        kq, kk, kqc, kwq, kwk = jax.random.split(key, 5)
        q = jax.random.normal(kq, (B, S, H), dtype=jnp.float32)
        k = jax.random.normal(kk, (B, S, H), dtype=jnp.float32)
        qc_score = jax.random.uniform(kqc, (B, S, S), dtype=jnp.float32)
        attn_mask = jnp.triu(jnp.ones((S, S), dtype=bool), k=1)
        key_padding_mask = jnp.zeros((B, S), dtype=bool)
        scale = 1.0 / np.sqrt(H)
        Wq = jax.random.normal(kwq, (H, H), dtype=jnp.float32) * scale
        Wk = jax.random.normal(kwk, (H, H), dtype=jnp.float32) * scale
        bq = jnp.zeros((H,), dtype=jnp.float32)
        bk = jnp.zeros((H,), dtype=jnp.float32)
        return {'q': q, 'k': k, 'attn_mask': attn_mask, 'key_padding_mask': key_padding_mask, 'qc_score': qc_score, 'Wq': Wq, 'bq': bq, 'Wk': Wk, 'bk': bk}
    _L0_xattn_all = _L0_xattn_setup()
    _L0_xattn_in = {k: v for k, v in _L0_xattn_all.items() if k in ('Wq', 'bq', 'Wk', 'bk')}
    del _L0_xattn_all

    def _L0_ffn_setup():
        import jax, jax.numpy as jnp
        import numpy as np
        HIDDEN = 256
        INTER = 1024
        SCALE = 64.0

        def fwht(x):
            orig_shape = x.shape
            n = orig_shape[-1]
            x = x.reshape(-1, n)
            h = 1
            while h < n:
                x = x.reshape(-1, n // (2 * h), 2, h)
                a, b = (x[:, :, 0, :], x[:, :, 1, :])
                x = jnp.stack([a + b, a - b], axis=2).reshape(-1, n)
                h *= 2
            return (x / jnp.sqrt(jnp.asarray(n, x.dtype))).reshape(orig_shape)
        key = jax.random.key(seed)
        ks = jax.random.split(key, 8)
        inp = jax.random.normal(ks[0], (4, 256, HIDDEN), dtype=jnp.float32)
        SU_ug = jnp.where(jax.random.bernoulli(ks[1], 0.5, (HIDDEN,)), 1.0, -1.0).astype(jnp.float32)
        SU_dp = jnp.where(jax.random.bernoulli(ks[2], 0.5, (INTER,)), 1.0, -1.0).astype(jnp.float32)
        Wscale_ug = jax.random.uniform(ks[3], (2 * INTER,), jnp.float32, 0.5, 1.5)
        Wscale_dp = jax.random.uniform(ks[4], (HIDDEN,), jnp.float32, 0.5, 1.5)
        W_up = jax.random.normal(ks[5], (INTER, HIDDEN), dtype=jnp.float32) * 0.02
        W_gate = jax.random.normal(ks[6], (INTER, HIDDEN), dtype=jnp.float32) * 0.02
        W_down = jax.random.normal(ks[7], (HIDDEN, INTER), dtype=jnp.float32) * 0.02
        return {'input': inp, 'SU_ug': SU_ug, 'SU_dp': SU_dp, 'Wscale_ug': Wscale_ug, 'Wscale_dp': Wscale_dp, 'W_up': W_up, 'W_gate': W_gate, 'W_down': W_down}
    _L0_ffn_all = _L0_ffn_setup()
    _L0_ffn_in = {k: v for k, v in _L0_ffn_all.items() if k in ('SU_ug', 'SU_dp', 'Wscale_ug', 'Wscale_dp', 'W_up', 'W_gate', 'W_down')}
    del _L0_ffn_all
    return {'x': x, 'ctx_512': ctx_512, 'mask_SxS2_bk1': mask_SxS2_bk1, 'mask_BxS2_bf0': mask_BxS2_bf0, 'L0_attn_q_w': _L0_attn_in['q_w'], 'L0_attn_q_b': _L0_attn_in['q_b'], 'L0_attn_k_w': _L0_attn_in['k_w'], 'L0_attn_k_b': _L0_attn_in['k_b'], 'L0_attn_v_w': _L0_attn_in['v_w'], 'L0_attn_v_b': _L0_attn_in['v_b'], 'L0_attn_o_w': _L0_attn_in['o_w'], 'L0_attn_o_b': _L0_attn_in['o_b'], 'L0_xattn_Wq': _L0_xattn_in['Wq'], 'L0_xattn_bq': _L0_xattn_in['bq'], 'L0_xattn_Wk': _L0_xattn_in['Wk'], 'L0_xattn_bk': _L0_xattn_in['bk'], 'L0_ffn_SU_ug': _L0_ffn_in['SU_ug'], 'L0_ffn_SU_dp': _L0_ffn_in['SU_dp'], 'L0_ffn_Wscale_ug': _L0_ffn_in['Wscale_ug'], 'L0_ffn_Wscale_dp': _L0_ffn_in['Wscale_dp'], 'L0_ffn_W_up': _L0_ffn_in['W_up'], 'L0_ffn_W_gate': _L0_ffn_in['W_gate'], 'L0_ffn_W_down': _L0_ffn_in['W_down']}

def reference(x, ctx_512, mask_SxS2_bk1, mask_BxS2_bf0, L0_attn_q_w, L0_attn_q_b, L0_attn_k_w, L0_attn_k_b, L0_attn_v_w, L0_attn_v_b, L0_attn_o_w, L0_attn_o_b, L0_xattn_Wq, L0_xattn_bq, L0_xattn_Wk, L0_xattn_bk, L0_ffn_SU_ug, L0_ffn_SU_dp, L0_ffn_Wscale_ug, L0_ffn_Wscale_dp, L0_ffn_W_up, L0_ffn_W_gate, L0_ffn_W_down):
    import jax
    import jax.numpy as jnp

    def _L0_attn_ref(hidden_states, q_w, q_b, k_w, k_b, v_w, v_b, o_w, o_b):
        import jax, jax.numpy as jnp
        import numpy as np
        HID = 256
        HEADS = 16
        HD = HID // HEADS
        EPS = 1e-06

        def _heads(x, b, s):
            return x.reshape(b, s, HEADS, HD).transpose(0, 2, 1, 3)
        b, s, _ = hidden_states.shape
        q = _heads(hidden_states @ q_w.T + q_b, b, s)
        k = _heads(hidden_states @ k_w.T + k_b, b, s)
        v = _heads(hidden_states @ v_w.T + v_b, b, s)
        qp = jax.nn.elu(q) + 1.0
        kp = jax.nn.elu(k) + 1.0
        kv = jnp.einsum('bhsd,bhse->bhde', kp, v)
        z = jnp.einsum('bhsd,bhd->bhs', qp, kp.sum(axis=2))[..., None]
        attn = jnp.einsum('bhsd,bhde->bhse', qp, kv) / (z + EPS)
        out = attn.transpose(0, 2, 1, 3).reshape(b, s, HID)
        return out @ o_w.T + o_b

    def _L0_xattn_ref(q, k, attn_mask, key_padding_mask, qc_score, Wq, bq, Wk, bk):
        import jax, jax.numpy as jnp
        import numpy as np
        B, S, H = (8, 256, 64)
        qp = jnp.einsum('bsh,oh->bso', q, Wq) + bq
        kp = jnp.einsum('bth,oh->bto', k, Wk) + bk
        scaling = jnp.asarray(float(H) ** (-0.5), dtype=qp.dtype)
        scores = jnp.einsum('bsh,bth->bst', qp, kp) * scaling
        scores = scores * qc_score
        mask = attn_mask[None, :, :] | key_padding_mask[:, None, :]
        scores = jnp.where(mask, -jnp.inf, scores)
        return jax.nn.softmax(scores, axis=-1)

    def _L0_ffn_ref(input, SU_ug, SU_dp, Wscale_ug, Wscale_dp, W_up, W_gate, W_down):
        import jax, jax.numpy as jnp
        import numpy as np
        HIDDEN = 256
        INTER = 1024
        SCALE = 64.0

        def fwht(x):
            orig_shape = x.shape
            n = orig_shape[-1]
            x = x.reshape(-1, n)
            h = 1
            while h < n:
                x = x.reshape(-1, n // (2 * h), 2, h)
                a, b = (x[:, :, 0, :], x[:, :, 1, :])
                x = jnp.stack([a + b, a - b], axis=2).reshape(-1, n)
                h *= 2
            return (x / jnp.sqrt(jnp.asarray(n, x.dtype))).reshape(orig_shape)
        n = SU_ug.shape[0]
        x = input.reshape(-1, n)
        x = fwht(x * SU_ug) / SCALE
        x_up = x @ W_up.T * (Wscale_ug[:INTER] * SCALE)
        x_gate = x @ W_gate.T * (Wscale_ug[INTER:] * SCALE)
        x = jax.nn.silu(x_gate) * x_up
        x = fwht(x * SU_dp) / SCALE
        x = x @ W_down.T * (Wscale_dp * SCALE)
        return x.reshape(input.shape)
    x = x + _L0_attn_ref(_layernorm(x, axis=-1), L0_attn_q_w, L0_attn_q_b, L0_attn_k_w, L0_attn_k_b, L0_attn_v_w, L0_attn_v_b, L0_attn_o_w, L0_attn_o_b)
    x = x + _L0_xattn_ref(ctx_512, ctx_512, mask_SxS2_bk1, mask_BxS2_bf0, _layernorm(x, axis=-1), L0_xattn_Wq, L0_xattn_bq, L0_xattn_Wk, L0_xattn_bk)
    x = x + _L0_ffn_ref(_layernorm(x, axis=-1), L0_ffn_SU_ug, L0_ffn_SU_dp, L0_ffn_Wscale_ug, L0_ffn_Wscale_dp, L0_ffn_W_up, L0_ffn_W_gate, L0_ffn_W_down)
    return x

_drawn_inputs = setup_inputs


def setup_inputs(seed=0):
    import zlib

    import numpy as np

    out = dict(_drawn_inputs(seed))
    spreads = {'L0_attn_q_b': (0.0, 0.8),
     'L0_attn_k_b': (0.0, 0.8),
     'L0_attn_v_b': (0.0, 0.1),
     'L0_attn_o_b': (0.0, 0.1),
     'L0_xattn_bq': (0.0, 0.8),
     'L0_xattn_bk': (0.0, 0.8)}
    factors = {'L0_attn_q_w': 3.333, 'L0_ffn_Wscale_dp': 3.316}
    for name, (base, spread) in spreads.items():
        noise = np.random.default_rng([zlib.crc32(name.encode()), seed]).standard_normal(out[name].shape)
        drawn = base * np.exp(spread * noise) if base else spread * noise
        out[name] = jnp.asarray(drawn.astype(out[name].dtype))
    for name, factor in factors.items():
        out[name] = (out[name] * factor).astype(out[name].dtype)
    return out
```

```python
import concourse.bass as bass
import numpy as np
from concourse import mybir
from contextlib import ExitStack

F32 = mybir.dt.float32
F32R = mybir.dt.float32r
BF16 = mybir.dt.bfloat16
U8 = mybir.dt.uint8
ALU = mybir.AluOpType
ACT = mybir.ActivationFunctionType
AX = mybir.AxisListType

P = 128
BATCH, SEQ, HID = 4, 256, 256
CTX = 64
HD = 16
INTER = 1024
TOK = BATCH * SEQ
TILES = TOK // P
HALVES = 2
HT = TILES // HALVES
HTOK = TOK // HALVES
BPH = BATCH // HALVES
FB = HID // P
JB = INTER // P
CB = TOK // 512
LN_EPS = 1e-5
Z_EPS = 1e-6
BANKS = 8
MASKED = 3.0e35
HIGHEST = 1.0e20

V_QB, V_SUG, V_SUD, V_WSUG, V_WSD, V_XB = 0, 2, 4, 12, 28, 30
V_COLS = 32


def hadamard(n):
    h = np.ones((1, 1), np.float32)
    while h.shape[0] < n:
        h = np.block([[h, h], [h, -h]])
    return h.astype(np.float32)


def schedule():
    order = []
    for c in range(CB):
        order += [(("qp", c), 2 * c), (("kp", c), 2 * c + 1)]
    order += [(("xnT", 0, f), 4 + f) for f in range(FB)]
    order += [(("score", b), 6 + b % 2) for b in range(2)]
    order += [(("q", 0, m), m) for m in range(FB)]
    order += [(("kv", t), 2 + t) for t in range(HT)]
    order += [(("score", b), 6 + b % 2) for b in range(2, 4)]
    order += [(("xnT", 1, f), f) for f in range(FB)]
    order += [(("state", b), 6 + b) for b in range(BPH)]
    order += [(("q", 1, m), 2 + m) for m in range(FB)]
    for b in range(BPH):
        order += [(("num", b), 4), (("z", b), 5)]
    order += [(("kv", HT + t), (0, 1, 2, 3)[t]) for t in range(HT)]
    order += [(("out", p), 6 + p % 2) for p in range(2)]
    order += [(("state", b), 4 + b % 2) for b in range(BPH, BATCH)]
    for b in range(BPH, BATCH):
        order += [(("num", b), 0 + 2 * (b % 2)), (("z", b), 1 + 2 * (b % 2))]
    order += [(("out", p), 6 + p % 2) for p in range(2, 4)]
    order += [(("wd", n), 2 + n) for n in range(4)]

    def tail(h):
        return ([(("x2T", h, f), 6 + f) for f in range(FB)] + [(("x3T", h, f), 6 + f) for f in range(FB)]
                + [(("xh", h, f), 6 + f) for f in range(FB)])

    order += tail(0)
    for h in range(HALVES):
        order += [(("y", h, o), 4 + o) for o in range(FB)]
        for j in range(JB):
            order += [(("gate", h, j), 2 * (j % 2)), (("up", h, j), 2 * (j % 2) + 1)]
            if h == 0 and j == 5:
                order += tail(1)
    return order


def decoder_kernel(nc, x, ctx_t, w_qkv, w_o, w_x, w_ug, w_d, vec, row, mask_ss, mask_key, const, out):
    order = schedule()
    bank_of, turn_of, uses = {}, {}, [0] * BANKS
    for group, bank in order:
        bank_of[group], turn_of[group] = bank, uses[bank]
        uses[bank] += 1

    stack = ExitStack()
    with stack:
        def sb(name, shape, dt=F32):
            return stack.enter_context(nc.sbuf_tensor(name, shape, dt))

        def sem(name):
            return stack.enter_context(nc.semaphore(name))

        xs = sb("x_res", [P, TILES, HID])
        wqkv = sb("wqkv", [P, FB, 3 * HID])
        wo = sb("wo", [P, FB, HID])
        wx = sb("wx", [CTX, 2 * CTX])
        ctxT = sb("ctxT", [CTX, TOK])
        vecs = sb("vecs", [P, V_COLS])
        rows = sb("rows", [P, 3 * HID])
        cst = sb("cst", [P, 2 * P + HID])
        ident, had, same_head = cst[:, 0:P], cst[:, P:2 * P], cst[:, 2 * P:2 * P + HID]
        mss = sb("mss", [P, SEQ // P, SEQ], U8)
        mkey = sb("mkey", [P, BATCH, SEQ], U8)
        bss = sb("bss", [P, SEQ // P, SEQ], BF16)
        bkey = sb("bkey", [P, BATCH, SEQ], BF16)
        mbias = sb("mbias", [P, TILES, SEQ], BF16)
        had_u = sb("had_u", [P, P], F32R)
        had_d = sb("had_d", [P, P], F32R)
        had_m = sb("had_m", [P, P], F32R)
        st = sb("st", [P, 2, TILES, 6])
        mv = sb("mv", [P, 3, TILES, 2])
        veps = sb("veps", [P, 3, TILES])
        rstd = sb("rstd", [P, 3, TILES])
        mhalf = sb("mhalf", [P, TILES])
        xn = sb("xn", [P, TILES, HID])
        xnT = sb("xnT", [P, FB, HTOK])
        eq = sb("eq", [P, 2, HTOK])
        rq = sb("rq", [P, 2, HTOK])
        qT = sb("qT", [P, FB, TOK])
        kt = sb("kt", [P, 2, HID])
        ek = sb("ek", [P, 2, HID])
        kp = sb("kp", [P, TILES, HID])
        VW = P + 2
        vx = sb("vx", [P, TILES, FB, VW])
        bd = sb("bd", [P, 2, 2, FB, P])
        zr = sb("zr", [P, 2, 2 * SEQ])
        qkp = sb("qkp", [P, 2, TOK])
        score = sb("score", [P, TILES, SEQ])
        low = sb("low", [P, TILES])
        psum_row = sb("psum_row", [P, TILES])
        rsum = sb("rsum", [P, TILES])
        stage = sb("stage", [P, 2, FB, 512])
        wug = sb("wug", [P, 2, FB, 2 * INTER], F32R)
        dpre = sb("dpre", [P, 2, JB, HID], F32R)
        wdh = sb("wdh", [P, 2, JB, HID], F32R)
        xs3 = sb("xs3", [P, 2, FB, HTOK], F32R)
        xh = sb("xh", [P, 2, HALVES, FB, HTOK], F32R)
        sg = rq
        wd_a, wd_b = qkp[:, :, :].rearrange("p a (n o) -> p (a n) o", o=HID), \
            stage[:, :, :, :].rearrange("p a f (n o) -> p (a f n) o", o=HID)
        hsp = dpre[:, :, :, :].rearrange("p l (n r) o -> p l n (r o)", r=2)
        HR = 4
        x2T = score[:, :, :].rearrange("p (h f a) s -> p h f (a s)", h=HALVES, f=FB)

        bank = [stack.enter_context(nc.psum_tensor(f"bank{i}", [P, 512], F32)) for i in range(BANKS)]
        full = [sem(f"bank_full{i}") for i in range(BANKS)]
        read = [sem(f"bank_read{i}") for i in range(BANKS)]

        def B(*group):
            return bank[bank_of[group]]

        def wait_full(eng, *group):
            eng.wait_ge(full[bank_of[group]], turn_of[group] + 1)

        def read_of(*group):
            return read[bank_of[group]]

        def wait_read(eng, *group):
            eng.wait_ge(read[bank_of[group]], turn_of[group] + 1)

        ld = {n: sem("ld_" + n) for n in ("x0", "x1", "ctx", "wx", "qkv", "wo", "vec", "row", "cst", "mss", "mkey",
                                          "ug0", "ug1", "ug2", "ug3", "wd", "out0", "out1", "out2", "out3")}
        names = ("had_ready mhalf_ready ones_ready mor mbias xb "
                 "stats1 aggr1 eps1 rstd1 xn1 stats2 aggr2 eps2 rstd2 stats3 aggr3 eps3 rstd3 xn3 "
                 "qkp_a qkp_d scores xnT_a xnT_d eq rq q kt ek rk kp vx bd bd_used z_eps z_inv attn x1 "
                 "sx logit prob rsum x2 ug_hi ug_lo fly fly_b fly_d pre_hi pre_lo wd_f wd_hi wd_lo wd_used "
                 "xs_hi xs_lo xh_hi xh_lo x2T silu h h_hi h_lo h_used y").split()
        s = {n: sem("s_" + n) for n in names}

        block = stack.enter_context(nc.Block())

        def h_slot_free(eng, n):
            m = n - HR
            if m >= 0 and m % JB == JB - 1:
                wait_full(eng, "y", m // JB, FB - 1)
            elif m >= 0:
                eng.wait_ge(s["h_used"], m + 1 - m // JB)

        @block.sync
        def _(sp):
            sp.dma_start(xs[:, 0:HT, :], x[:, 0:HT, :]).then_inc(ld["x0"], 16)
            sp.dma_start(cst[:, :], const).then_inc(ld["cst"], 16)
            sp.dma_start(wqkv[:, :, :], w_qkv).then_inc(ld["qkv"], 16)
            sp.dma_start(xs[:, HT:TILES, :], x[:, HT:TILES, :]).then_inc(ld["x1"], 16)
            sp.dma_start(wo[:, :, :], w_o).then_inc(ld["wo"], 16)
            for c in range(4):
                if c >= 2:
                    sp.wait_ge(s["ug_hi"], c - 1)
                    sp.wait_ge(s["ug_lo"], c - 1)
                sp.dma_start(stage[:, c % 2, :, :], w_ug[:, :, c * 512:(c + 1) * 512]).then_inc(ld[f"ug{c}"], 16)
            for b in range(BATCH):
                wait_full(sp, "score", b)
            sp.dma_start(wd_a, w_d).then_inc(ld["wd"], 16)
            for h in range(HALVES):
                for o in range(FB):
                    wait_read(sp, "y", h, o)
                    sp.dma_start(out[:, o, h * HTOK:(h + 1) * HTOK], x2T[:, h, o, :]).then_inc(ld[f"out{FB * h + o}"], 16)
            for n in range(4):
                sp.wait_ge(ld[f"out{n}"], 16)

        @block.gpsimd
        def _(pool):
            g = nc.gpsimd
            g.memset(mhalf[:, :], -0.5).then_inc(s["mhalf_ready"], 1)
            g.memset(vx[:, :, :, P:VW], 1.0).then_inc(s["ones_ready"], 1)
            pool.wait_ge(s["mhalf_ready"], 1)

            def rstd_of(n, h):
                pool.wait_ge(s[f"aggr{n}"], HT * (h + 1))
                a, z = h * HT, (h + 1) * HT
                g.tensor_scalar(veps[:, n - 1, a:z], mv[:, n - 1, a:z, 1], LN_EPS, None, ALU.add).then_inc(s[f"eps{n}"], 1)
                pool.wait_ge(s[f"eps{n}"], h + 1)
                g.tensor_tensor(rstd[:, n - 1, a:z], veps[:, n - 1, a:z], mhalf[:, a:z], ALU.pow).then_inc(s[f"rstd{n}"], 1)

            def relu_k(t):
                pool.wait_ge(s["ek"], t + 1)
                g.tensor_scalar(kt[:, t % 2, :], kt[:, t % 2, :], 0.0, None, ALU.max).then_inc(s["rk"], 1)

            def add_ob(t):
                pool.wait_ge(s["xn1"], t + 1)
                g.tensor_tensor(xs[:, t, :], xs[:, t, :], rows[:, 2 * HID:3 * HID], ALU.add).then_inc(s["xb"], 1)

            def mask_bias():
                pool.wait_ge(s["mor"], 2)
                for i in range(SEQ // P):
                    g.tensor_tensor(mbias[:, i:TILES:2, :], bss[:, i:i + 1, :].to_broadcast([P, BATCH, SEQ]),
                                    bkey[:, :, :], ALU.add).then_inc(s["mbias"], 1)

            def ug_lo(c):
                pool.wait_ge(s["ug_hi"], c + 1)
                g.tensor_tensor(wug[:, 1, :, c * 512:(c + 1) * 512], stage[:, c % 2, :, :],
                                wug[:, 0, :, c * 512:(c + 1) * 512].bitcast(F32), ALU.subtract).then_inc(s["ug_lo"], 1)

            rstd_of(1, 0)
            rstd_of(1, 1)
            pool.wait_ge(ld["row"], 16)
            for t in range(HT):
                add_ob(t)
            for t in range(HT):
                relu_k(t)
            for t in range(HT, TILES):
                add_ob(t)
            mask_bias()
            ug_lo(0)
            for t in range(HT, TILES):
                relu_k(t)
            ug_lo(1)
            rstd_of(2, 0)
            ug_lo(2)
            rstd_of(3, 0)
            ug_lo(3)
            pool.wait_ge(ld["wd"], 16)
            pool.wait_ge(s["ug_lo"], 4)
            src, dst = wd_a, wd_b
            for stage_no, step in enumerate((4, 2, 1)):
                if stage_no:
                    pool.wait_ge(s["fly"], 2 * stage_no)
                a = src.rearrange("p (u two v) o -> p u two (v o)", two=2, v=step)
                d = dst.rearrange("p (u two v) o -> p u two (v o)", two=2, v=step)
                g.tensor_tensor(d[:, :, 0, :], a[:, :, 0, :], a[:, :, 1, :], ALU.add).then_inc(s["fly"], 1)
                g.tensor_tensor(d[:, :, 1, :], a[:, :, 0, :], a[:, :, 1, :], ALU.subtract).then_inc(s["fly"], 1)
                src, dst = dst, src
            pool.wait_ge(s["fly"], 6)
            pool.wait_ge(s["pre_hi"], 1)
            g.tensor_tensor(dpre[:, 1, :, :], wd_b, dpre[:, 0, :, :].bitcast(F32), ALU.subtract).then_inc(s["pre_lo"], 1)
            rstd_of(2, 1)
            rstd_of(3, 1)
            for n in range(HALVES * JB):
                pool.wait_ge(s["h_hi"], n + 1)
                h_slot_free(pool, n)
                g.tensor_tensor(hsp[:, 1, n % HR, :], sg[:, n % 2, :], hsp[:, 0, n % HR, :].bitcast(F32),
                                ALU.subtract).then_inc(s["h_lo"], 1)

        @block.scalar
        def _(act):
            a = nc.scalar
            act.dma_start(ctxT[:, :], ctx_t).then_inc(ld["ctx"], 16)
            act.dma_start(wx[:, :], w_x).then_inc(ld["wx"], 16)
            act.dma_start(vecs[:, :], vec).then_inc(ld["vec"], 16)
            act.dma_start(rows[:, :], row.partition_broadcast(P)).then_inc(ld["row"], 16)
            act.dma_start(mss[:, :, :], mask_ss).then_inc(ld["mss"], 16)
            act.dma_start(mkey[:, :, :], mask_key.partition_broadcast(P)).then_inc(ld["mkey"], 16)
            act.wait_ge(ld["vec"], 16)
            for c in range(CB):
                wait_full(act, "kp", c)
                a.activation(qkp[0:CTX, 1, c * 512:(c + 1) * 512], B("kp", c)[0:CTX, :], ACT.Identity,
                             bias=vecs[0:CTX, V_XB + 1:V_XB + 2]).then_inc(read_of("kp", c), 1)

            def xnT_evac(h):
                wait_full(act, "xnT", h, 0)
                a.copy(xnT[:, 0, :], B("xnT", h, 0)[:, :]).then_inc(read_of("xnT", h, 0), 1)

            def scores(b):
                wait_full(act, "score", b)
                a.mul(score[:, 2 * b:2 * b + 2, :].rearrange("p t s -> p (t s)"), B("score", b)[:, :],
                      -float(CTX) ** -0.5).then_inc(read_of("score", b), 1)

            def exp_q(h, m):
                n = FB * h + m
                wait_full(act, "q", h, m)
                if n >= 2:
                    act.wait_ge(s["q"], n - 1)
                a.activation(eq[:, n % 2, :], B("q", h, m)[:, :], ACT.Exp,
                             bias=vecs[:, V_QB + m:V_QB + m + 1]).then_inc(s["eq"], 1)

            def exp_k(t):
                act.wait_ge(s["kt"], t + 1)
                if t >= 2:
                    act.wait_ge(s["kp"], t - 1)
                a.activation(ek[:, t % 2, :], kt[:, t % 2, :], ACT.Exp).then_inc(s["ek"], 1)

            def z_eps(b):
                wait_full(act, "z", b)
                if b >= 2:
                    wait_read(act, "num", b - 2)
                a.activation(zr[:, b % 2, :], B("z", b)[:, :], ACT.Copy, bias=Z_EPS).then_inc(read_of("z", b), 1)

            def ug_hi(c):
                act.wait_ge(ld[f"ug{c}"], 16)
                a.copy(wug[:, 0, :, c * 512:(c + 1) * 512], stage[:, c % 2, :, :]).then_inc(s["ug_hi"], 1)

            def prob(t):
                act.wait_ge(s["logit"], t + 1)
                a.activation(score[:, t, :], score[:, t, :], ACT.Exp, bias=low[:, t:t + 1], scale=-1.0,
                             accum_out=psum_row[:, t:t + 1]).then_inc(s["prob"], 1)

            def tail_hi(h):
                for f in range(FB):
                    wait_full(act, "x3T", h, f)
                    if h:
                        wait_full(act, "xh", 0, 1)
                    a.activation(xs3[:, 0, f, :], B("x3T", h, f)[:, :], ACT.Copy,
                                 scale=vecs[:, V_SUG + f:V_SUG + f + 1]).then_inc(s["xs_hi"], 1)
                for f in range(FB):
                    wait_full(act, "xh", h, f)
                    a.copy(xh[:, 0, h, f, :], B("xh", h, f)[:, :]).then_inc(s["xh_hi"], 1)

            xnT_evac(0)
            scores(0)
            scores(1)
            exp_q(0, 0)
            exp_q(0, 1)
            for t in range(HT):
                exp_k(t)
            scores(2)
            scores(3)
            xnT_evac(1)
            exp_q(1, 0)
            exp_q(1, 1)
            z_eps(0)
            z_eps(1)
            ug_hi(0)
            for t in range(HT, TILES):
                exp_k(t)
            ug_hi(1)
            z_eps(2)
            z_eps(3)
            for t in range(HT):
                prob(t)
            ug_hi(2)
            ug_hi(3)
            act.wait_ge(s["fly"], 6)
            a.copy(dpre[:, 0, :, :], wd_b).then_inc(s["pre_hi"], 1)
            tail_hi(0)
            for n in range(4):
                wait_read(act, "wd", n)
                a.copy(wdh[:, 0, 2 * n:2 * n + 2, :], wd_a[:, 2 * n:2 * n + 2, :]).then_inc(s["wd_hi"], 1)
            for t in range(HT, TILES):
                prob(t)
            for h in range(HALVES):
                for j in range(JB):
                    n = JB * h + j
                    if n >= 2:
                        act.wait_ge(s["h_lo"], n - 1)
                    wait_full(act, "gate", h, j)
                    a.activation(sg[:, n % 2, :], B("gate", h, j)[:, :], ACT.Silu,
                                 scale=vecs[:, V_WSUG + JB + j:V_WSUG + JB + j + 1]).then_inc(read_of("gate", h, j), 1)
                    wait_read(act, "up", h, j)
                    h_slot_free(act, n)
                    a.copy(hsp[:, 0, n % HR, :], sg[:, n % 2, :]).then_inc(s["h_hi"], 1)
                    if h == 0 and j == 5:
                        tail_hi(1)

        @block.vector
        def _(dve):
            v = nc.vector

            def norm_stats(n, t):
                v.bn_stats(st[:, t % 2, t, :], xs[:, t, :]).then_inc(s[f"stats{n}"], 1)

            def norm_aggr(n, t):
                dve.wait_ge(s[f"stats{n}"], t + 1)
                v.bn_aggr(mv[:, n - 1, t, :], st[:, t % 2, t, :]).then_inc(s[f"aggr{n}"], 1)

            def normalise(n, t):
                dve.wait_ge(s[f"rstd{n}"], t // HT + 1)
                if n == 1:
                    dve.wait_ge(s["aggr1"], t + 1)
                v.tensor_scalar(xn[:, t, :], xs[:, t, :], mv[:, n - 1, t, 0:1], rstd[:, n - 1, t:t + 1],
                                ALU.subtract, ALU.mult).then_inc(s[f"xn{n}"], 1)

            def ln1(h):
                dve.wait_ge(ld[f"x{h}"], 16)
                for t in range(h * HT, (h + 1) * HT):
                    norm_stats(1, t)
                for t in range(h * HT, (h + 1) * HT):
                    norm_aggr(1, t)
                for t in range(h * HT, (h + 1) * HT):
                    normalise(1, t)

            def xnT_evac(h):
                wait_full(dve, "xnT", h, 1)
                v.tensor_copy(xnT[:, 1, :], B("xnT", h, 1)[:, :]).then_inc(read_of("xnT", h, 1), 1)

            def elu_q(h, m):
                n = FB * h + m
                dve.wait_ge(s["eq"], n + 1)
                v.tensor_scalar(rq[:, n % 2, :], B("q", h, m)[:, :], vecs[:, V_QB + m:V_QB + m + 1], 0.0,
                                ALU.add, ALU.max).then_inc(read_of("q", h, m), 1)
                wait_read(dve, "q", h, m)
                v.scalar_tensor_tensor(qT[:, m, h * HTOK:(h + 1) * HTOK], eq[:, n % 2, :], 1.0, rq[:, n % 2, :],
                                       ALU.min, ALU.add).then_inc(s["q"], 1)

            def kv(t):
                wait_full(dve, "kv", t)
                if t >= 2:
                    dve.wait_ge(s["kp"], t - 1)
                v.tensor_tensor(kt[:, t % 2, :], B("kv", t)[:, 0:HID], rows[:, 0:HID], ALU.add).then_inc(s["kt"], 1)
                v.tensor_tensor(vx[:, t, :, 0:P], B("kv", t)[:, HID:2 * HID].rearrange("p (g e) -> p g e", g=FB),
                                rows[:, HID:2 * HID].rearrange("p (g e) -> p g e", g=FB),
                                ALU.add).then_inc(read_of("kv", t), 1)

            def elu_k(t):
                dve.wait_ge(s["rk"], t + 1)
                v.scalar_tensor_tensor(kp[:, t, :], ek[:, t % 2, :], 1.0, kt[:, t % 2, :],
                                       ALU.min, ALU.add).then_inc(s["kp"], 1)

            def diagonal(b):
                wait_full(dve, "state", b)
                if b >= 2:
                    wait_full(dve, "z", b - 2)
                got = B("state", b)[:, 0:FB * VW].rearrange("p (g e) -> p g e", g=FB)
                mask = same_head.rearrange("p (g e) -> p g e", g=FB)
                v.tensor_tensor(bd[:, b % 2, 0, :, :], got[:, :, 0:P], mask, ALU.mult)
                v.tensor_tensor(bd[:, b % 2, 1, :, :], got[:, :, P:P + 1].to_broadcast([P, FB, P]), mask,
                                ALU.mult).then_inc(read_of("state", b), 1)

            def attend(b):
                wait_read(dve, "z", b)
                v.reciprocal(zr[:, b % 2, :], zr[:, b % 2, :]).then_inc(s["z_inv"], 1)
                wait_full(dve, "num", b)
                dve.wait_ge(s["z_inv"], b + 1)
                v.tensor_tensor(qT[:, :, b * SEQ:(b + 1) * SEQ], B("num", b)[:, :].rearrange("p (g s) -> p g s", g=FB),
                                zr[:, b % 2, :].rearrange("p (g s) -> p g s", g=FB), ALU.mult)\
                    .then_inc(read_of("num", b), 1)

            def add_attn(p):
                wait_full(dve, "out", p)
                dve.wait_ge(s["xb"], 2 * p + 2)
                v.tensor_tensor(xs[:, 2 * p:2 * p + 2, :], B("out", p)[:, :].rearrange("p (t d) -> p t d", t=2),
                                xs[:, 2 * p:2 * p + 2, :], ALU.add).then_inc(read_of("out", p), 1)

            def mask_bias():
                dve.wait_ge(ld["mss"], 16)
                v.tensor_scalar(bss[:, :, :], mss[:, :, :], MASKED, None, ALU.mult).then_inc(s["mor"], 1)
                dve.wait_ge(ld["mkey"], 16)
                v.tensor_scalar(bkey[:, :, :], mkey[:, :, :], MASKED, None, ALU.mult).then_inc(s["mor"], 1)

            def xattn(h):
                a, z = h * HT, (h + 1) * HT
                for t in range(a, z):
                    wait_read(dve, "out", t // 2)
                    norm_stats(2, t)
                for t in range(a, z):
                    norm_aggr(2, t)
                for t in range(a, z):
                    dve.wait_ge(s["aggr2"], t + 1)
                    wait_read(dve, "score", t // 2)
                    v.scalar_tensor_tensor(score[:, t, :], xs[:, t, :], mv[:, 1, t, 0:1], score[:, t, :],
                                           ALU.subtract, ALU.mult).then_inc(s["sx"], 1)
                dve.wait_ge(s["rstd2"], h + 1)
                for t in range(a, z):
                    dve.wait_ge(s["sx"], t + 1)
                    dve.wait_ge(s["mbias"], 2)
                    v.tensor_tensor_reduce(out=score[:, t, :], in0=score[:, t, :], in1=mbias[:, t, :],
                                           scale=rstd[:, 1, t:t + 1], scalar=HIGHEST, op0=ALU.add, op1=ALU.min,
                                           accum_out=low[:, t:t + 1]).then_inc(s["logit"], 1)
                for t in range(a, z):
                    dve.wait_ge(s["prob"], t + 1)
                    v.reciprocal(rsum[:, t:t + 1], psum_row[:, t:t + 1]).then_inc(s["rsum"], 1)
                for t in range(a, z):
                    dve.wait_ge(s["rsum"], t + 1)
                    v.scalar_tensor_tensor(xs[:, t, :], score[:, t, :], rsum[:, t:t + 1], xs[:, t, :],
                                           ALU.mult, ALU.add).then_inc(s["x2"], 1)
                for t in range(a, z):
                    dve.wait_ge(s["x2"], t + 1)
                    norm_stats(3, t)
                for t in range(a, z):
                    norm_aggr(3, t)
                for t in range(a, z):
                    normalise(3, t)

            def tail(h):
                for f in range(FB):
                    wait_full(dve, "x2T", h, f)
                    v.tensor_copy(x2T[:, h, f, :], B("x2T", h, f)[:, :]).then_inc(read_of("x2T", h, f), 1)
                for f in range(FB):
                    dve.wait_ge(s["xs_hi"], FB * h + f + 1)
                    v.scalar_tensor_tensor(xs3[:, 1, f, :], B("x3T", h, f)[:, :], vecs[:, V_SUG + f:V_SUG + f + 1],
                                           xs3[:, 0, f, :].bitcast(F32), ALU.mult, ALU.subtract)\
                        .then_inc(read_of("x3T", h, f), 1)
                for f in range(FB):
                    dve.wait_ge(s["xh_hi"], FB * h + f + 1)
                    v.tensor_tensor(xh[:, 1, h, f, :], B("xh", h, f)[:, :], xh[:, 0, h, f, :].bitcast(F32),
                                    ALU.subtract).then_inc(read_of("xh", h, f), 1)

            ln1(0)
            dve.wait_ge(ld["vec"], 16)
            for c in range(CB):
                wait_full(dve, "qp", c)
                v.tensor_scalar(qkp[0:CTX, 0, c * 512:(c + 1) * 512], B("qp", c)[0:CTX, :],
                                vecs[0:CTX, V_XB:V_XB + 1], None, ALU.add).then_inc(read_of("qp", c), 1)
            xnT_evac(0)
            dve.wait_ge(ld["cst"], 16)
            v.tensor_scalar(had_u[:, :], had, float(HID) ** -0.5, None, ALU.mult).then_inc(s["had_ready"], 1)
            v.tensor_scalar(had_m[:, :], had, -float(HID) ** -0.5, None, ALU.mult).then_inc(s["had_ready"], 1)
            v.tensor_scalar(had_d[:, :], had, float(INTER) ** -0.5, None, ALU.mult).then_inc(s["had_ready"], 1)
            ln1(1)
            elu_q(0, 0)
            elu_q(0, 1)
            dve.wait_ge(ld["row"], 16)
            kv(0)
            kv(1)
            for t in range(2, HT):
                elu_k(t - 2)
                kv(t)
            elu_k(2)
            elu_k(3)
            xnT_evac(1)
            diagonal(0)
            diagonal(1)
            elu_q(1, 0)
            elu_q(1, 1)
            mask_bias()
            attend(0)
            attend(1)
            kv(4)
            kv(5)
            for t in range(HT + 2, TILES):
                elu_k(t - 2)
                kv(t)
            elu_k(6)
            elu_k(7)
            add_attn(0)
            add_attn(1)
            diagonal(2)
            diagonal(3)
            attend(2)
            attend(3)
            xattn(0)
            add_attn(2)
            add_attn(3)
            tail(0)
            for n in range(4):
                wait_full(dve, "wd", n)
                dve.wait_ge(s["pre_lo"], 1)
                for i in range(2):
                    ins = v.tensor_scalar(wd_a[:, 2 * n + i, :], B("wd", n)[:, i * HID:(i + 1) * HID],
                                          vecs[:, V_SUD + 2 * n + i:V_SUD + 2 * n + i + 1], None, ALU.mult)
                    if i == 1:
                        ins.then_inc(read_of("wd", n), 1)
            for n in range(4):
                dve.wait_ge(s["wd_hi"], n + 1)
                v.tensor_tensor(wdh[:, 1, 2 * n:2 * n + 2, :], wd_a[:, 2 * n:2 * n + 2, :],
                                wdh[:, 0, 2 * n:2 * n + 2, :].bitcast(F32), ALU.subtract).then_inc(s["wd_lo"], 1)
            xattn(1)
            for h in range(HALVES):
                for j in range(JB):
                    n = JB * h + j
                    wait_read(dve, "gate", h, j)
                    wait_full(dve, "up", h, j)
                    v.scalar_tensor_tensor(sg[:, n % 2, :], B("up", h, j)[:, :], vecs[:, V_WSUG + j:V_WSUG + j + 1],
                                           sg[:, n % 2, :], ALU.mult, ALU.mult).then_inc(read_of("up", h, j), 1)
                    if h == 0 and j == 5:
                        tail(1)
                for o in range(FB):
                    wait_full(dve, "y", h, o)
                    v.scalar_tensor_tensor(x2T[:, h, o, :], B("y", h, o)[:, :], vecs[:, V_WSD + o:V_WSD + o + 1],
                                           x2T[:, h, o, :], ALU.mult, ALU.add).then_inc(read_of("y", h, o), 1)

        @block.tensor
        def _(pe):
            mm = nc.tensor.matmul
            last_down = [0]

            def take(*group):
                if turn_of[group]:
                    pe.wait_ge(read_of(*group), turn_of[group])
                return B(*group)

            def done(ins, *group):
                ins.then_inc(full[bank_of[group]], 1)

            def project(name, c):
                dst = take(name, c)
                w = wx[:, 0:CTX] if name == "qp" else wx[:, CTX:2 * CTX]
                done(mm(dst[0:CTX, :], w, ctxT[:, c * 512:(c + 1) * 512], start=True, stop=True), name, c)

            def scores(b):
                wait_read(pe, "qp", b // 2)
                wait_read(pe, "kp", b // 2)
                dst = take("score", b)
                for i in range(2):
                    ins = mm(dst[:, i * SEQ:(i + 1) * SEQ], qkp[0:CTX, 0, b * SEQ + i * P:b * SEQ + (i + 1) * P],
                             qkp[0:CTX, 1, b * SEQ:(b + 1) * SEQ], start=True, stop=True)
                done(ins, "score", b)

            def turn(name, h, src):
                for f in range(FB):
                    dst = take(name, h, f)
                    for i in range(HT):
                        ins = nc.tensor.transpose(dst[:, i * P:(i + 1) * P], src[:, h * HT + i, f * P:(f + 1) * P], ident)
                    done(ins, name, h, f)

            def norm1(h):
                pe.wait_ge(s["xn1"], HT * (h + 1))
                turn("xnT", h, xn)

            def q_proj(h):
                for f in range(FB):
                    wait_read(pe, "xnT", h, f)
                for m in range(FB):
                    dst = take("q", h, m)
                    for k in range(FB):
                        ins = mm(dst[:, :], wqkv[:, k, m * P:(m + 1) * P], xnT[:, k, :], start=(k == 0), stop=(k == FB - 1))
                    done(ins, "q", h, m)

            def kv_proj(h):
                for t in range(h * HT, (h + 1) * HT):
                    dst = take("kv", t)
                    for k in range(FB):
                        ins = mm(dst[:, :], xnT[:, k, t % HT * P:(t % HT + 1) * P], wqkv[:, k, HID:3 * HID],
                                 start=(k == 0), stop=(k == FB - 1))
                    done(ins, "kv", t)

            def state(b):
                pe.wait_ge(s["kp"], 2 * b + 2)
                wait_read(pe, "kv", 2 * b)
                wait_read(pe, "kv", 2 * b + 1)
                dst = take("state", b)
                for g in range(FB):
                    for i in range(2):
                        ins = mm(dst[:, g * VW:(g + 1) * VW], kp[:, 2 * b + i, g * P:(g + 1) * P], vx[:, 2 * b + i, g, :],
                                 start=(i == 0), stop=(i == 1))
                done(ins, "state", b)

            def attend(b):
                pe.wait_ge(s["q"], FB * (b // BPH) + FB)
                wait_read(pe, "state", b)
                for part, name in enumerate(("num", "z")):
                    dst = take(name, b)
                    for g in range(FB):
                        ins = mm(dst[:, g * SEQ:(g + 1) * SEQ], bd[:, b % 2, part, g, :], qT[:, g, b * SEQ:(b + 1) * SEQ],
                                 start=True, stop=True)
                    done(ins, name, b)

            def o_proj(p):
                wait_read(pe, "num", p)
                dst = take("out", p)
                for i in range(2):
                    for k in range(FB):
                        ins = mm(dst[:, i * HID:(i + 1) * HID], qT[:, k, (2 * p + i) * P:(2 * p + i + 1) * P], wo[:, k, :],
                                 start=(k == 0), stop=(k == FB - 1))
                done(ins, "out", p)

            def w_down():
                pe.wait_ge(s["pre_lo"], 1)
                pe.wait_ge(s["had_ready"], 3)
                for n in range(4):
                    dst = take("wd", n)
                    for part in range(2):
                        ins = mm(dst[:, :], had_d[:, :], dpre[:, part, 2 * n:2 * n + 2, :].rearrange("p n o -> p (n o)"),
                                 start=(part == 0), stop=(part == 1))
                    done(ins, "wd", n)

            def tail(h):
                pe.wait_ge(s["x2"], HT * (h + 1))
                turn("x2T", h, xs)
                pe.wait_ge(s["xn3"], HT * (h + 1))
                turn("x3T", h, xn)
                for f in range(FB):
                    wait_read(pe, "x3T", h, f)
                for f in range(FB):
                    dst = take("xh", h, f)
                    for k in range(FB):
                        for part in range(2):
                            ins = mm(dst[:, :], (had_m if f and k else had_u)[:, :], xs3[:, part, k, :],
                                     start=(k == 0 and part == 0), stop=(k == FB - 1 and part == 1))
                    done(ins, "xh", h, f)

            PARTS = ((1, 0), (0, 1), (0, 0))

            def ffn_up(h, j):
                for name, at in (("gate", INTER), ("up", 0)):
                    dst = take(name, h, j)
                    for k in range(FB):
                        for i, (a, b) in enumerate(PARTS):
                            ins = mm(dst[:, :], wug[:, a, k, at + j * P:at + (j + 1) * P], xh[:, b, h, k, :],
                                     start=(k == 0 and i == 0), stop=(k == FB - 1 and i == 2))
                    done(ins, name, h, j)

            def ffn_down(h, j):
                n = JB * h + j
                pe.wait_ge(s["h_lo"], n + 1)
                for o in range(FB):
                    if j == 0:
                        take("y", h, o)
                    for i, (a, b) in enumerate(PARTS):
                        ins = mm(B("y", h, o)[:, :], wdh[:, a, j, o * P:(o + 1) * P], hsp[:, b, n % HR, :],
                                 start=(j == 0 and i == 0), stop=(j == JB - 1 and i == 2))
                    if j == JB - 1:
                        done(ins, "y", h, o)
                if j < JB - 1:
                    ins.then_inc(s["h_used"], 1)

            pe.wait_ge(ld["ctx"], 16)
            pe.wait_ge(ld["wx"], 16)
            for c in range(CB):
                project("qp", c)
                project("kp", c)
            pe.wait_ge(ld["cst"], 16)
            norm1(0)
            scores(0)
            scores(1)
            pe.wait_ge(ld["qkv"], 16)
            q_proj(0)
            kv_proj(0)
            scores(2)
            scores(3)
            norm1(1)
            pe.wait_ge(s["ones_ready"], 1)
            state(0)
            state(1)
            q_proj(1)
            attend(0)
            attend(1)
            kv_proj(1)
            pe.wait_ge(ld["wo"], 16)
            o_proj(0)
            o_proj(1)
            state(2)
            state(3)
            attend(2)
            attend(3)
            o_proj(2)
            o_proj(3)
            w_down()
            tail(0)
            for c in range(4):
                pe.wait_ge(s["ug_lo"], c + 1)
            for n in range(4):
                pe.wait_ge(s["wd_lo"], n + 1)
            for h in range(HALVES):
                for j in range(JB):
                    ffn_up(h, j)
                    if j >= 2:
                        ffn_down(h, j - 2)
                    if h == 0 and j == 5:
                        tail(1)
                ffn_down(h, JB - 2)
                ffn_down(h, JB - 1)


def kernel(**inputs):
    import concourse.bacc as _bacc
    from concourse.bass_utils import run_bass_kernel_spmd as _run

    a = {k: np.asarray(v) for k, v in inputs.items()}

    def blocks(w):
        return w.reshape(-1, P, w.shape[-1]).transpose(1, 0, 2)

    def columns(w):
        return w.reshape(-1, P).T

    zero = np.zeros((P - CTX, 2), np.float32)
    eye, ones = np.eye(P, dtype=np.float32), np.ones((HD, HD), np.float32)
    arrays = {
        "x": blocks(a["x"].reshape(TOK, HID)),
        "ctx_t": a["ctx_512"].reshape(TOK, CTX).T,
        "w_qkv": blocks(np.concatenate([a["L0_attn_q_w"], a["L0_attn_k_w"], a["L0_attn_v_w"]]).T),
        "w_o": blocks(a["L0_attn_o_w"].T),
        "w_x": np.concatenate([a["L0_xattn_Wq"], a["L0_xattn_Wk"]]).T,
        "w_ug": blocks(np.concatenate([a["L0_ffn_W_up"], a["L0_ffn_W_gate"]]).T),
        "w_d": blocks(a["L0_ffn_W_down"].T),
        "vec": np.concatenate([columns(a[n]) for n in ("L0_attn_q_b", "L0_ffn_SU_ug", "L0_ffn_SU_dp",
                                                       "L0_ffn_Wscale_ug", "L0_ffn_Wscale_dp")]
                              + [np.concatenate([np.stack([a["L0_xattn_bq"], a["L0_xattn_bk"]], 1), zero])], 1),
        "row": np.concatenate([a[n] for n in ("L0_attn_k_b", "L0_attn_v_b", "L0_attn_o_b")]),
        "mask_ss": blocks(a["mask_SxS2_bk1"]),
        "mask_key": a["mask_BxS2_bf0"],
        "const": np.concatenate([eye, hadamard(P), np.tile(np.kron(np.eye(P // HD, dtype=np.float32), ones), (1, FB))], 1),
    }
    nc = _bacc.Bacc("TRN2", target_bir_lowering=False, num_devices=1)
    sent, args = {}, []
    for name, arr in arrays.items():
        arr = np.ascontiguousarray(arr)
        sent[f"in_{name}"] = arr
        args.append(nc.dram_tensor(f"in_{name}", arr.shape, mybir.dt.from_np(arr.dtype), kind="ExternalInput").ap())
    args.append(nc.dram_tensor("out_0", (P, FB, TOK), F32, kind="ExternalOutput").ap())
    decoder_kernel(nc, *args)
    got = _run(nc, [sent], core_ids=[0]).results[0]["out_0"]
    return np.ascontiguousarray(got.transpose(2, 1, 0)).reshape(BATCH, SEQ, HID)
```

```python
import concourse.bass as bass
import numpy as np
from concourse import mybir
from contextlib import ExitStack

F32 = mybir.dt.float32
F32R = mybir.dt.float32r
BF16 = mybir.dt.bfloat16
U8 = mybir.dt.uint8
ALU = mybir.AluOpType
ACT = mybir.ActivationFunctionType
AX = mybir.AxisListType

P = 128
BATCH, SEQ, HID = 4, 256, 256
CTX = 64
HD = 16
INTER = 1024
TOK = BATCH * SEQ
TILES = TOK // P
HALVES = 2
HT = TILES // HALVES
HTOK = TOK // HALVES
BPH = BATCH // HALVES
FB = HID // P
JB = INTER // P
CB = TOK // 512
LN_EPS = 1e-5
Z_EPS = 1e-6
BANKS = 8
WARM = 17
MASKED = 3.0e35
HIGHEST = 1.0e20

V_QB, V_SUG, V_SUD, V_WSUG, V_WSD, V_XB = 0, 2, 4, 12, 28, 30
V_COLS = 32
UG_ORDER = (0, 2, 1, 3)


TAIL_AT = {3: "x2T", 4: "x3T", 6: "xh"}


def hadamard(n):
    h = np.ones((1, 1), np.float32)
    while h.shape[0] < n:
        h = np.block([[h, h], [h, -h]])
    return h.astype(np.float32)


def schedule():
    order = [(("xnT", 0, 0), 0), (("xnT", 0, 1), 1), (("qp", 0), 2), (("kp", 0), 3), (("q", 0, 0), 4), (("q", 0, 1), 5),
             (("kv", 0), 6), (("kv", 1), 7), (("kv", 2), 0), (("kv", 3), 1), (("xnT", 1, 0), 4), (("xnT", 1, 1), 5),
             (("qp", 1), 2), (("kp", 1), 3), (("state", 0), 6), (("state", 1), 7), (("q", 1, 0), 0), (("q", 1, 1), 1),
             (("z", 0), 4), (("z", 1), 5), (("num", 0), 2), (("num", 1), 3), (("score", 0), 6), (("kv", 4), 7),
             (("kv", 5), 0), (("rz", 0), 1), (("rz", 1), 4), (("kv", 6), 5), (("kv", 7), 6), (("score", 1), 7),
             (("out", 0), 2), (("out", 1), 3), (("state", 2), 0), (("state", 3), 1), (("score", 2), 4),
             (("score", 3), 5), (("z", 2), 2), (("z", 3), 3), (("num", 2), 0), (("num", 3), 1),
             (("wd", 0), 6), (("wd", 1), 7), (("wd", 2), 4), (("wd", 3), 5), (("rz", 2), 2), (("rz", 3), 3),
             (("out", 2), 0), (("out", 3), 1),
             (("x2T", 0, 0), 2), (("x2T", 0, 1), 3), (("x3T", 0, 0), 0), (("x3T", 0, 1), 1),
             (("xh", 0, 0), 2), (("xh", 0, 1), 3)]
    for h in range(HALVES):
        for j in range(JB):
            order += [(("gate", h, j), 2 * (j % 2)), (("up", h, j), 2 * (j % 2) + 1)]
            if j == 2:
                order += [(("y", h, o), 4 + o) for o in range(FB)]
            if h == 0 and j in TAIL_AT:
                order += [((TAIL_AT[j], 1, f), 6 + f) for f in range(FB)]
    return order


def decoder_kernel(nc, x, ctx_t, w_qkv, w_o, w_x, w_ug, w_d, vec, row, mask_ss, mask_key, const, out):
    order = schedule()
    bank_of, turn_of, uses = {}, {}, [0] * BANKS
    for group, bank in order:
        bank_of[group], turn_of[group] = bank, uses[bank]
        uses[bank] += 1

    stack = ExitStack()
    with stack:
        def sb(name, shape, dt=F32):
            return stack.enter_context(nc.sbuf_tensor(name, shape, dt))

        def sem(name):
            return stack.enter_context(nc.semaphore(name))

        xs = sb("x_res", [P, TILES, HID])
        wqkv = sb("wqkv", [P, 2, FB, 3 * HID], F32R)
        wo = sb("wo", [P, FB, HID])
        wx = sb("wx", [CTX, 2 * CTX])
        ctx_buf = sb("ctx_buf", [P, TOK])
        ctxT = ctx_buf[0:CTX, :]
        vecs = sb("vecs", [P, V_COLS])
        rows = sb("rows", [P, 3 * HID])
        HPB = P // HD
        cst = sb("cst", [P, 2 * P + HID + FB * HPB])
        ident, had, same_head = cst[:, 0:P], cst[:, P:2 * P], cst[:, 2 * P:2 * P + HID]
        head_of = cst[:, 2 * P + HID:]
        mss = sb("mss", [P, SEQ // P, SEQ], U8)
        mkey = sb("mkey", [P, BATCH, SEQ], U8)
        bkey = ctx_buf[:, 0:BATCH * SEQ // 2].bitcast(BF16).rearrange("p (b s) -> p b s", s=SEQ)
        bss = ctx_buf[:, BATCH * SEQ // 2:BATCH * SEQ // 2 + SEQ].bitcast(BF16).rearrange("p (i s) -> p i s", s=SEQ)
        mbias = sb("mbias", [P, TILES, SEQ], BF16)
        junk = mbias[:, 0:2, :].rearrange("p t s -> p (t s)")
        had_u = sb("had_u", [P, P], F32R)
        had_d = sb("had_d", [P, P], F32R)
        had_m = sb("had_m", [P, P], F32R)
        st = sb("st", [P, 2, TILES, 6])
        mv = sb("mv", [P, 3, TILES, 2])
        veps = sb("veps", [P, 3, TILES])
        rstd = sb("rstd", [P, 3, TILES])
        mhalf = sb("mhalf", [P, TILES])
        exp_first = sb("exp_first", [P, TILES])
        xn = sb("xn", [P, HT, HID])
        eq = sb("eq", [P, 2, HTOK])
        qT = sb("qT", [P, FB, TOK])
        kt = sb("kt", [P, 2, HID])
        ek = sb("ek", [P, 2, HID])
        rk = sb("rk", [P, 2, HID])
        kp = sb("kp", [P, HT, HID])
        VW = P + 2
        vx = sb("vx", [P, HT, FB, VW])
        bd = sb("bd", [P, BATCH, FB, P])
        ks = sb("ks", [P, BATCH, FB, HPB])
        ze = sb("ze", [P, TILES, FB * HPB])
        zi = sb("zi", [P, TILES, FB * HPB])
        zr = sb("zr", [P, 2, 2 * SEQ])
        qkp = sb("qkp", [P, 2, TOK])
        score = sb("score", [P, TILES, SEQ])
        low = sb("low", [P, TILES])
        psum_row = sb("psum_row", [P, TILES])
        rsum = sb("rsum", [P, TILES])
        stage = sb("stage", [P, 2, FB, 512])
        wug = sb("wug", [P, 2, FB, 2 * INTER], F32R)
        dpre = sb("dpre", [P, 2, JB, HID], F32R)
        wdh = sb("wdh", [P, 2, JB, HID], F32R)
        xs3 = sb("xs3", [P, 2, FB, HTOK], F32R)
        wd_raw = sb("wd_raw", [P, JB, HID])
        wd_alt = sb("wd_alt", [P, JB, HID])
        xh = sb("xh", [P, 2, HALVES, FB, HTOK], F32R)
        sg = eq
        wd_a, wd_b = wd_raw[:, :, :], wd_alt[:, :, :]
        qkv_raw = stage[:, :, :, :].rearrange("p a f n -> p (a f n)")[:, 0:FB * 3 * HID]\
            .rearrange("p (f n) -> p f n", f=FB)
        hsp = dpre[:, :, :, :].rearrange("p l (n r) o -> p l n (r o)", r=2)
        HR = 4
        x2T = score[:, :, :].rearrange("p (h f a) s -> p h f (a s)", h=HALVES, f=FB)

        bank = [stack.enter_context(nc.psum_tensor(f"bank{i}", [P, 512], F32)) for i in range(BANKS)]
        full = [sem(f"bank_full{i}") for i in range(BANKS)]
        read = [sem(f"bank_read{i}") for i in range(BANKS)]

        def B(*group):
            return bank[bank_of[group]]

        def wait_full(eng, *group):
            eng.wait_ge(full[bank_of[group]], turn_of[group] + 1)

        def read_of(*group):
            return read[bank_of[group]]

        def wait_read(eng, *group):
            eng.wait_ge(read[bank_of[group]], turn_of[group] + 1)

        ld = {n: sem("ld_" + n) for n in ("x0", "x1", "ctx", "wx", "qkv", "wo", "vec", "row", "cst", "mss", "mkey",
                                          "ug0", "ug1", "ug2", "ug3", "wd", "out0", "out1", "out2", "out3")}
        names = ("had_ready junk_ready w_hi w_lo mhalf_ready ones_ready mor mbias xb "
                 "stats1 aggr1 eps1 rstd1 xn1 stats2 aggr2 eps2 rstd2 stats3 aggr3 eps3 rstd3 xn3 "
                 "qkp_a qkp_d scores xnT_hi eq q kt ek rk kp z_spread z_inv "
                 "sx logit prob rsum x2 ug_hi ug_lo_v ug_lo_p fly fly_b fly_d pre_hi pre_lo wd_f wd_hi wd_lo wd_used "
                 "xs_hi xs_lo xh_hi xh_lo x2T silu h h_hi h_lo h_used y").split()
        s = {n: sem("s_" + n) for n in names}

        block = stack.enter_context(nc.Block())

        def h_slot_free(eng, n):
            m = n - HR
            if m >= 0 and m % JB == JB - 1:
                wait_full(eng, "y", m // JB, FB - 1)
            elif m >= 0:
                eng.wait_ge(s["h_used"], m + 1 - m // JB)

        @block.sync
        def _(sp):
            sp.dma_start(xs[:, 0:HT, :], x[:, 0:HT, :]).then_inc(ld["x0"], 16)
            sp.dma_start(qkv_raw, w_qkv).then_inc(ld["qkv"], 16)
            sp.dma_start(xs[:, HT:TILES, :], x[:, HT:TILES, :]).then_inc(ld["x1"], 16)
            sp.dma_start(wd_a, w_d).then_inc(ld["wd"], 16)
            sp.dma_start(rows[:, :], row.partition_broadcast(P)).then_inc(ld["row"], 16)
            sp.dma_start(mss[:, :, :], mask_ss).then_inc(ld["mss"], 16)
            sp.dma_start(mkey[:, :, :], mask_key.partition_broadcast(P)).then_inc(ld["mkey"], 16)
            sp.dma_start(wo[:, :, :], w_o).then_inc(ld["wo"], 16)
            for n, c in enumerate(UG_ORDER):
                if n < 2:
                    sp.wait_ge(s["w_hi"], 2)
                    sp.wait_ge(s["w_lo"], 2)
                else:
                    sp.wait_ge(s["ug_hi"], n - 1)
                    sp.wait_ge(s["ug_lo_v"], n - 1)
                sp.dma_start(stage[:, n % 2, :, :], w_ug[:, :, c * 512:(c + 1) * 512]).then_inc(ld[f"ug{n}"], 16)
            for h in range(HALVES):
                for o in range(FB):
                    wait_read(sp, "y", h, o)
                    sp.dma_start(out[:, o, h * HTOK:(h + 1) * HTOK], x2T[:, h, o, :]).then_inc(ld[f"out{FB * h + o}"], 16)
            for n in range(4):
                sp.wait_ge(ld[f"out{n}"], 16)

        @block.gpsimd
        def _(pool):
            g = nc.gpsimd
            g.memset(mhalf[:, :], -0.5).then_inc(s["mhalf_ready"], 1)
            g.memset(junk[:, :], 0.0).then_inc(s["junk_ready"], 1)
            g.memset(vx[:, :, :, P:VW], 1.0).then_inc(s["ones_ready"], 1)
            pool.wait_ge(s["mhalf_ready"], 1)

            def rstd_of(n, h):
                pool.wait_ge(s[f"aggr{n}"], HT * (h + 1))
                a, z = h * HT, (h + 1) * HT
                g.tensor_scalar(veps[:, n - 1, a:z], mv[:, n - 1, a:z, 1], LN_EPS, None, ALU.add).then_inc(s[f"eps{n}"], 1)
                pool.wait_ge(s[f"eps{n}"], h + 1)
                g.tensor_tensor(rstd[:, n - 1, a:z], veps[:, n - 1, a:z], mhalf[:, a:z], ALU.pow).then_inc(s[f"rstd{n}"], 1)

            def add_ob(t):
                pool.wait_ge(s["xn1"], t + 1)
                g.tensor_tensor(xs[:, t, :], xs[:, t, :], rows[:, 2 * HID:3 * HID], ALU.add).then_inc(s["xb"], 1)

            def mask_bias():
                pool.wait_ge(s["mor"], 2)
                for i in range(SEQ // P):
                    g.tensor_tensor(mbias[:, i:TILES:2, :], bss[:, i:i + 1, :].to_broadcast([P, BATCH, SEQ]),
                                    bkey[:, :, :], ALU.add).then_inc(s["mbias"], 1)

            def ug_lo(n):
                c = UG_ORDER[n]
                pool.wait_ge(s["ug_hi"], n + 1)
                g.tensor_tensor(wug[:, 1, :, c * 512:(c + 1) * 512], stage[:, n % 2, :, :],
                                wug[:, 0, :, c * 512:(c + 1) * 512].bitcast(F32), ALU.subtract).then_inc(s["ug_lo_p"], 1)

            def pre_lo(n):
                part = slice(n * JB // 2, (n + 1) * JB // 2)
                pool.wait_ge(s["pre_hi"], n + 1)
                g.tensor_tensor(dpre[:, 1, part, :], wd_b[:, part, :], dpre[:, 0, part, :].bitcast(F32),
                                ALU.subtract).then_inc(s["pre_lo"], 1)

            def butterfly(stage_no):
                if stage_no:
                    pool.wait_ge(s["fly"], 2 * stage_no)
                src, dst = ((wd_a, wd_b), (wd_b, wd_a))[stage_no % 2]
                src, dst = (w.rearrange("p (u two v) o -> p u two (v o)", two=2, v=JB >> (stage_no + 1)) for w in (src, dst))
                g.tensor_tensor(dst[:, :, 0, :], src[:, :, 0, :], src[:, :, 1, :], ALU.add).then_inc(s["fly"], 1)
                g.tensor_tensor(dst[:, :, 1, :], src[:, :, 0, :], src[:, :, 1, :], ALU.subtract).then_inc(s["fly"], 1)

            rstd_of(1, 0)
            pool.wait_ge(ld["wd"], 16)
            butterfly(0)
            rstd_of(1, 1)
            butterfly(1)
            butterfly(2)
            pool.wait_ge(ld["row"], 16)
            for t in range(HT):
                add_ob(t)
            pre_lo(0)
            pre_lo(1)
            mask_bias()
            ug_lo(2)
            for t in range(HT, TILES):
                add_ob(t)
            rstd_of(2, 0)
            ug_lo(3)
            rstd_of(3, 0)
            rstd_of(2, 1)
            for n in range(HALVES * JB):
                pool.wait_ge(s["h_hi"], n + 1)
                h_slot_free(pool, n)
                g.tensor_tensor(hsp[:, 1, n % HR, :], sg[:, n % 2, :], hsp[:, 0, n % HR, :].bitcast(F32),
                                ALU.subtract).then_inc(s["h_lo"], 1)
                if n == 0:
                    rstd_of(3, 1)

        @block.scalar
        def _(act):
            a = nc.scalar
            act.dma_start(cst[:, :], const).then_inc(ld["cst"], 16)
            act.dma_start(ctxT[:, :], ctx_t).then_inc(ld["ctx"], 16)
            act.dma_start(wx[:, :], w_x).then_inc(ld["wx"], 16)
            act.dma_start(vecs[:, :], vec).then_inc(ld["vec"], 16)
            act.wait_ge(s["mhalf_ready"], 1)
            a.activation(exp_first[:, :], mhalf[:, :], ACT.Exp)

            def kp_evac(c):
                wait_full(act, "kp", c)
                a.activation(qkp[0:CTX, 1, c * 512:(c + 1) * 512], B("kp", c)[0:CTX, :], ACT.Identity,
                             bias=vecs[0:CTX, V_XB + 1:V_XB + 2]).then_inc(read_of("kp", c), 1)

            def w_hi(n):
                act.wait_ge(ld["qkv"], 16)
                cols = (slice(0, HID), slice(HID, 3 * HID))[n]
                a.copy(wqkv[:, 0, :, cols], qkv_raw[:, :, cols]).then_inc(s["w_hi"], 1)

            def xnT_hi(h):
                for f in range(FB):
                    wait_full(act, "xnT", h, f)
                    a.copy(xs3[:, 0, f, :], B("xnT", h, f)[:, :]).then_inc(s["xnT_hi"], 1)

            def scores(b):
                wait_full(act, "score", b)
                a.mul(score[:, 2 * b:2 * b + 2, :].rearrange("p t s -> p (t s)"), B("score", b)[:, :],
                      -float(CTX) ** -0.5).then_inc(read_of("score", b), 1)

            def exp_q(h, m):
                n = FB * h + m
                wait_full(act, "q", h, m)
                if n >= 2:
                    act.wait_ge(s["q"], n - 1)
                a.activation(eq[:, n % 2, :], B("q", h, m)[:, :], ACT.Exp,
                             bias=vecs[:, V_QB + m:V_QB + m + 1]).then_inc(s["eq"], 1)

            def exp_k(t):
                act.wait_ge(s["kt"], t + 1)
                if t >= 2:
                    act.wait_ge(s["kp"], t - 1)
                a.activation(ek[:, t % 2, :], kt[:, t % 2, :], ACT.Exp).then_inc(s["ek"], 1)
                a.activation(rk[:, t % 2, :], kt[:, t % 2, :], ACT.Relu).then_inc(s["rk"], 1)

            def z_spread(b):
                act.wait_ge(s["z_inv"], b + 1)
                if b >= 2:
                    wait_read(act, "num", b - 2)
                a.copy(zr[:, b % 2, :].rearrange("p (n d) -> p n d", d=HD),
                       zi[:, 2 * b:2 * b + 2, :].rearrange("p t h -> p (t h)").unsqueeze(2)
                       .to_broadcast([P, 2 * FB * HPB, HD])).then_inc(s["z_spread"], 1)

            def rz_evac(b):
                wait_full(act, "rz", b)
                a.copy(zr[:, b % 2, :], B("rz", b)[:, :]).then_inc(read_of("rz", b), 1)

            def mask_value():
                act.wait_ge(ld["mss"], 16)
                a.mul(bss[:, :, :], mss[:, :, :], MASKED).then_inc(s["mor"], 1)
                act.wait_ge(ld["mkey"], 16)
                a.mul(bkey[:, :, :], mkey[:, :, :], MASKED).then_inc(s["mor"], 1)

            def wd_hi(n):
                wait_full(act, "wd", n)
                for i in range(2):
                    a.activation(wdh[:, 0, 2 * n + i, :], B("wd", n)[:, i * HID:(i + 1) * HID], ACT.Copy,
                                 scale=vecs[:, V_SUD + 2 * n + i:V_SUD + 2 * n + i + 1]).then_inc(s["wd_hi"], 1)

            def pre_hi(n):
                part = slice(n * JB // 2, (n + 1) * JB // 2)
                act.wait_ge(s["fly"], 6)
                a.copy(dpre[:, 0, part, :], wd_b[:, part, :]).then_inc(s["pre_hi"], 1)

            def ug_hi(n):
                c = UG_ORDER[n]
                act.wait_ge(ld[f"ug{n}"], 16)
                a.copy(wug[:, 0, :, c * 512:(c + 1) * 512], stage[:, n % 2, :, :]).then_inc(s["ug_hi"], 1)

            def prob(t):
                act.wait_ge(s["logit"], t + 1)
                a.activation(score[:, t, :], score[:, t, :], ACT.Exp, bias=low[:, t:t + 1], scale=-1.0,
                             accum_out=psum_row[:, t:t + 1]).then_inc(s["prob"], 1)

            def x2T_evac(h):
                for f in range(FB):
                    wait_full(act, "x2T", h, f)
                    a.copy(x2T[:, h, f, :], B("x2T", h, f)[:, :]).then_inc(read_of("x2T", h, f), 1)

            def x3T_hi(h):
                for f in range(FB):
                    wait_full(act, "x3T", h, f)
                    if h:
                        wait_full(act, "xh", 0, 1)
                    a.activation(xs3[:, 0, f, :], B("x3T", h, f)[:, :], ACT.Copy,
                                 scale=vecs[:, V_SUG + f:V_SUG + f + 1]).then_inc(s["xs_hi"], 1)

            def xh_hi(h):
                for f in range(FB):
                    wait_full(act, "xh", h, f)
                    a.copy(xh[:, 0, h, f, :], B("xh", h, f)[:, :]).then_inc(s["xh_hi"], 1)

            w_hi(0)
            w_hi(1)
            xnT_hi(0)
            act.wait_ge(ld["vec"], 16)
            kp_evac(0)
            exp_q(0, 0)
            exp_q(0, 1)
            for t in range(HT):
                exp_k(t)
            xnT_hi(1)
            kp_evac(1)
            ug_hi(0)
            mask_value()
            exp_q(1, 0)
            exp_q(1, 1)
            ug_hi(1)
            pre_hi(0)
            z_spread(0)
            z_spread(1)
            scores(0)
            pre_hi(1)
            exp_k(4)
            exp_k(5)
            rz_evac(0)
            rz_evac(1)
            ug_hi(2)
            exp_k(6)
            exp_k(7)
            scores(1)
            ug_hi(3)
            scores(2)
            scores(3)
            wd_hi(0)
            wd_hi(1)
            for t in range(HT):
                prob(t)
            z_spread(2)
            z_spread(3)
            wd_hi(2)
            wd_hi(3)
            rz_evac(2)
            rz_evac(3)
            x2T_evac(0)
            x3T_hi(0)
            xh_hi(0)
            for t in range(HT, TILES):
                prob(t)
            for h in range(HALVES):
                for j in range(JB):
                    n = JB * h + j
                    if n >= 2:
                        act.wait_ge(s["h_lo"], n - 1)
                    wait_full(act, "gate", h, j)
                    a.activation(sg[:, n % 2, :], B("gate", h, j)[:, :], ACT.Silu,
                                 scale=vecs[:, V_WSUG + JB + j:V_WSUG + JB + j + 1]).then_inc(read_of("gate", h, j), 1)
                    wait_read(act, "up", h, j)
                    h_slot_free(act, n)
                    a.copy(hsp[:, 0, n % HR, :], sg[:, n % 2, :]).then_inc(s["h_hi"], 1)
                    if h == 0 and j in TAIL_AT:
                        {"x2T": x2T_evac, "x3T": x3T_hi, "xh": xh_hi}[TAIL_AT[j]](1)

        @block.vector
        def _(dve):
            v = nc.vector

            def norm_stats(n, t):
                v.bn_stats(st[:, t % 2, t, :], xs[:, t, :]).then_inc(s[f"stats{n}"], 1)

            def norm_aggr(n, t):
                dve.wait_ge(s[f"stats{n}"], t + 1)
                v.bn_aggr(mv[:, n - 1, t, :], st[:, t % 2, t, :]).then_inc(s[f"aggr{n}"], 1)

            def normalise(n, t):
                dve.wait_ge(s[f"rstd{n}"], t // HT + 1)
                if n == 1:
                    dve.wait_ge(s["aggr1"], t + 1)
                v.tensor_scalar(xn[:, t % HT, :], xs[:, t, :], mv[:, n - 1, t, 0:1], rstd[:, n - 1, t:t + 1],
                                ALU.subtract, ALU.mult).then_inc(s[f"xn{n}"], 1)

            def qp_evac(c):
                wait_full(dve, "qp", c)
                v.tensor_scalar(qkp[0:CTX, 0, c * 512:(c + 1) * 512], B("qp", c)[0:CTX, :],
                                vecs[0:CTX, V_XB:V_XB + 1], None, ALU.add).then_inc(read_of("qp", c), 1)

            def ln1(h, between=None):
                dve.wait_ge(ld[f"x{h}"], 16)
                for t in range(h * HT, (h + 1) * HT):
                    norm_stats(1, t)
                for t in range(h * HT, (h + 1) * HT):
                    norm_aggr(1, t)
                if between:
                    between()
                for t in range(h * HT, (h + 1) * HT):
                    normalise(1, t)

            def w_lo(n):
                dve.wait_ge(s["w_hi"], n + 1)
                cols = (slice(0, HID), slice(HID, 3 * HID))[n]
                v.tensor_tensor(wqkv[:, 1, :, cols], qkv_raw[:, :, cols], wqkv[:, 0, :, cols].bitcast(F32),
                                ALU.subtract).then_inc(s["w_lo"], 1)

            def ug_lo(n):
                c = UG_ORDER[n]
                dve.wait_ge(s["ug_hi"], n + 1)
                v.tensor_tensor(wug[:, 1, :, c * 512:(c + 1) * 512], stage[:, n % 2, :, :],
                                wug[:, 0, :, c * 512:(c + 1) * 512].bitcast(F32), ALU.subtract).then_inc(s["ug_lo_v"], 1)

            def xnT_lo(h):
                for f in range(FB):
                    dve.wait_ge(s["xnT_hi"], FB * h + f + 1)
                    v.tensor_tensor(xs3[:, 1, f, :], B("xnT", h, f)[:, :], xs3[:, 0, f, :].bitcast(F32),
                                    ALU.subtract).then_inc(read_of("xnT", h, f), 1)

            def elu_q(h, m):
                n = FB * h + m
                dve.wait_ge(s["eq"], n + 1)
                into = qT[:, m, h * HTOK:(h + 1) * HTOK]
                v.tensor_scalar(into, B("q", h, m)[:, :], vecs[:, V_QB + m:V_QB + m + 1], 0.0,
                                ALU.add, ALU.max).then_inc(read_of("q", h, m), 1)
                wait_read(dve, "q", h, m)
                v.scalar_tensor_tensor(into, eq[:, n % 2, :], 1.0, into, ALU.min, ALU.add).then_inc(s["q"], 1)

            def kv(t):
                wait_full(dve, "kv", t)
                if t >= 2:
                    dve.wait_ge(s["kp"], t - 1)
                v.tensor_tensor(kt[:, t % 2, :], B("kv", t)[:, 0:HID], rows[:, 0:HID], ALU.add).then_inc(s["kt"], 1)
                v.tensor_tensor(vx[:, t % HT, :, 0:P], B("kv", t)[:, HID:2 * HID].rearrange("p (g e) -> p g e", g=FB),
                                rows[:, HID:2 * HID].rearrange("p (g e) -> p g e", g=FB),
                                ALU.add).then_inc(read_of("kv", t), 1)

            def elu_k(t):
                dve.wait_ge(s["rk"], t + 1)
                v.scalar_tensor_tensor(kp[:, t % HT, :], ek[:, t % 2, :], 1.0, rk[:, t % 2, :],
                                       ALU.min, ALU.add).then_inc(s["kp"], 1)

            def diagonal(b):
                wait_full(dve, "state", b)
                got = B("state", b)[:, 0:FB * VW].rearrange("p (g e) -> p g e", g=FB)
                v.tensor_tensor(bd[:, b, :, :], got[:, :, 0:P], same_head.rearrange("p (g e) -> p g e", g=FB), ALU.mult)
                v.tensor_tensor(ks[:, b, :, :], got[:, :, P:P + 1].to_broadcast([P, FB, HPB]),
                                head_of.rearrange("p (g h) -> p g h", g=FB), ALU.mult).then_inc(read_of("state", b), 1)

            def z_inverse(b):
                wait_full(dve, "z", b)
                two = slice(2 * b, 2 * b + 2)
                v.tensor_scalar(ze[:, two, :].rearrange("p t h -> p (t h)"), B("z", b)[:, 0:2 * FB * HPB], Z_EPS, None,
                                ALU.add).then_inc(read_of("z", b), 1)
                wait_read(dve, "z", b)
                v.reciprocal(zi[:, two, :], ze[:, two, :]).then_inc(s["z_inv"], 1)

            def attend(b):
                wait_full(dve, "num", b)
                wait_read(dve, "rz", b)
                v.tensor_tensor(qT[:, :, b * SEQ:(b + 1) * SEQ], B("num", b)[:, :].rearrange("p (g s) -> p g s", g=FB),
                                zr[:, b % 2, :].rearrange("p (g s) -> p g s", g=FB), ALU.mult)\
                    .then_inc(read_of("num", b), 1)

            def add_attn(p):
                wait_full(dve, "out", p)
                dve.wait_ge(s["xb"], 2 * p + 2)
                v.tensor_tensor(xs[:, 2 * p:2 * p + 2, :], B("out", p)[:, :].rearrange("p (t d) -> p t d", t=2),
                                xs[:, 2 * p:2 * p + 2, :], ALU.add).then_inc(read_of("out", p), 1)

            def ln2(h):
                a, z = h * HT, (h + 1) * HT
                for t in range(a, z):
                    wait_read(dve, "out", t // 2)
                    norm_stats(2, t)
                for t in range(a, z):
                    norm_aggr(2, t)

            def times_score(h):
                a, z = h * HT, (h + 1) * HT
                for t in range(a, z):
                    dve.wait_ge(s["aggr2"], t + 1)
                    wait_read(dve, "score", t // 2)
                    v.scalar_tensor_tensor(score[:, t, :], xs[:, t, :], mv[:, 1, t, 0:1], score[:, t, :],
                                           ALU.subtract, ALU.mult).then_inc(s["sx"], 1)

            def logits(h):
                a, z = h * HT, (h + 1) * HT
                dve.wait_ge(s["rstd2"], h + 1)
                for t in range(a, z):
                    dve.wait_ge(s["sx"], t + 1)
                    dve.wait_ge(s["mbias"], 2)
                    v.tensor_tensor_reduce(out=score[:, t, :], in0=score[:, t, :], in1=mbias[:, t, :],
                                           scale=rstd[:, 1, t:t + 1], scalar=HIGHEST, op0=ALU.add, op1=ALU.min,
                                           accum_out=low[:, t:t + 1]).then_inc(s["logit"], 1)

            def softmax(h):
                a, z = h * HT, (h + 1) * HT
                for t in range(a, z):
                    dve.wait_ge(s["prob"], t + 1)
                    v.reciprocal(rsum[:, t:t + 1], psum_row[:, t:t + 1]).then_inc(s["rsum"], 1)
                for t in range(a, z):
                    dve.wait_ge(s["rsum"], t + 1)
                    v.scalar_tensor_tensor(xs[:, t, :], score[:, t, :], rsum[:, t:t + 1], xs[:, t, :],
                                           ALU.mult, ALU.add).then_inc(s["x2"], 1)
                for t in range(a, z):
                    dve.wait_ge(s["x2"], t + 1)
                    norm_stats(3, t)
                for t in range(a, z):
                    norm_aggr(3, t)

            def ln3(h):
                for t in range(h * HT, (h + 1) * HT):
                    normalise(3, t)

            def x3T_lo(h):
                for f in range(FB):
                    dve.wait_ge(s["xs_hi"], FB * h + f + 1)
                    v.scalar_tensor_tensor(xs3[:, 1, f, :], B("x3T", h, f)[:, :], vecs[:, V_SUG + f:V_SUG + f + 1],
                                           xs3[:, 0, f, :].bitcast(F32), ALU.mult, ALU.subtract)\
                        .then_inc(read_of("x3T", h, f), 1)

            def xh_lo(h):
                for f in range(FB):
                    dve.wait_ge(s["xh_hi"], FB * h + f + 1)
                    v.tensor_tensor(xh[:, 1, h, f, :], B("xh", h, f)[:, :], xh[:, 0, h, f, :].bitcast(F32),
                                    ALU.subtract).then_inc(read_of("xh", h, f), 1)

            def wd_lo(n):
                dve.wait_ge(s["wd_hi"], 2 * n + 2)
                for i in range(2):
                    ins = v.scalar_tensor_tensor(
                        wdh[:, 1, 2 * n + i, :], B("wd", n)[:, i * HID:(i + 1) * HID],
                        vecs[:, V_SUD + 2 * n + i:V_SUD + 2 * n + i + 1], wdh[:, 0, 2 * n + i, :].bitcast(F32),
                        ALU.mult, ALU.subtract)
                ins.then_inc(read_of("wd", n), 1)

            ln1(0, between=lambda: w_lo(0))
            w_lo(1)
            xnT_lo(0)
            dve.wait_ge(ld["vec"], 16)
            qp_evac(0)
            ln1(1)
            dve.wait_ge(ld["cst"], 16)
            v.tensor_scalar(had_u[:, :], had, float(HID) ** -0.5, None, ALU.mult).then_inc(s["had_ready"], 1)
            v.tensor_scalar(had_m[:, :], had, -float(HID) ** -0.5, None, ALU.mult).then_inc(s["had_ready"], 1)
            v.tensor_scalar(had_d[:, :], had, float(INTER) ** -0.5, None, ALU.mult).then_inc(s["had_ready"], 1)
            elu_q(0, 0)
            elu_q(0, 1)
            dve.wait_ge(ld["row"], 16)
            kv(0)
            kv(1)
            for t in range(2, HT):
                elu_k(t - 2)
                kv(t)
            elu_k(2)
            elu_k(3)
            xnT_lo(1)
            qp_evac(1)
            diagonal(0)
            diagonal(1)
            ug_lo(0)
            elu_q(1, 0)
            elu_q(1, 1)
            z_inverse(0)
            z_inverse(1)
            ug_lo(1)
            kv(4)
            kv(5)
            attend(0)
            attend(1)
            elu_k(4)
            kv(6)
            elu_k(5)
            kv(7)
            add_attn(0)
            elu_k(6)
            elu_k(7)
            add_attn(1)
            ln2(0)
            diagonal(2)
            diagonal(3)
            times_score(0)
            logits(0)
            z_inverse(2)
            z_inverse(3)
            softmax(0)
            attend(2)
            attend(3)
            ln3(0)
            add_attn(2)
            add_attn(3)
            x3T_lo(0)
            ln2(1)
            xh_lo(0)
            times_score(1)
            logits(1)
            for n in range(4):
                wd_lo(n)
            for h in range(HALVES):
                for j in range(JB):
                    n = JB * h + j
                    wait_read(dve, "gate", h, j)
                    wait_full(dve, "up", h, j)
                    v.scalar_tensor_tensor(sg[:, n % 2, :], B("up", h, j)[:, :], vecs[:, V_WSUG + j:V_WSUG + j + 1],
                                           sg[:, n % 2, :], ALU.mult, ALU.mult).then_inc(read_of("up", h, j), 1)
                    if n == 0:
                        softmax(1)
                    if n == 1:
                        ln3(1)
                    if h == 0 and j in TAIL_AT:
                        {"x2T": lambda h: None, "x3T": x3T_lo, "xh": xh_lo}[TAIL_AT[j]](1)
                for o in range(FB):
                    wait_full(dve, "y", h, o)
                    v.scalar_tensor_tensor(x2T[:, h, o, :], B("y", h, o)[:, :], vecs[:, V_WSD + o:V_WSD + o + 1],
                                           x2T[:, h, o, :], ALU.mult, ALU.add).then_inc(read_of("y", h, o), 1)

        @block.tensor
        def _(pe):
            mm = nc.tensor.matmul
            last_down = [0]

            def take(*group):
                if turn_of[group]:
                    pe.wait_ge(read_of(*group), turn_of[group])
                return B(*group)

            def done(ins, *group):
                ins.then_inc(full[bank_of[group]], 1)

            def project(name, c):
                dst = take(name, c)
                w = wx[:, 0:CTX] if name == "qp" else wx[:, CTX:2 * CTX]
                done(mm(dst[0:CTX, :], w, ctxT[:, c * 512:(c + 1) * 512], start=True, stop=True), name, c)

            def scores(b):
                wait_read(pe, "qp", b // 2)
                wait_read(pe, "kp", b // 2)
                dst = take("score", b)
                for i in range(2):
                    ins = mm(dst[:, i * SEQ:(i + 1) * SEQ], qkp[0:CTX, 0, b * SEQ + i * P:b * SEQ + (i + 1) * P],
                             qkp[0:CTX, 1, b * SEQ:(b + 1) * SEQ], start=True, stop=True)
                done(ins, "score", b)

            def turn(name, h, src):
                for f in range(FB):
                    dst = take(name, h, f)
                    for i in range(HT):
                        ins = nc.tensor.transpose(dst[:, i * P:(i + 1) * P], src[:, i, f * P:(f + 1) * P], ident)
                    done(ins, name, h, f)

            def norm1(h):
                pe.wait_ge(s["xn1"], HT * (h + 1))
                turn("xnT", h, xn)

            def q_proj(h):
                for f in range(FB):
                    wait_read(pe, "xnT", h, f)
                for m in range(FB):
                    dst = take("q", h, m)
                    for k in range(FB):
                        for i, (a, b) in enumerate(PARTS):
                            ins = mm(dst[:, :], wqkv[:, a, k, m * P:(m + 1) * P], xs3[:, b, k, :],
                                     start=(k == 0 and i == 0), stop=(k == FB - 1 and i == 2))
                    done(ins, "q", h, m)

            def kv_proj(t):
                dst = take("kv", t)
                for k in range(FB):
                    for i, (a, b) in enumerate(PARTS):
                        ins = mm(dst[:, :], xs3[:, b, k, t % HT * P:(t % HT + 1) * P], wqkv[:, a, k, HID:3 * HID],
                                 start=(k == 0 and i == 0), stop=(k == FB - 1 and i == 2))
                done(ins, "kv", t)

            def state(b):
                pe.wait_ge(s["kp"], 2 * b + 2)
                wait_read(pe, "kv", 2 * b)
                wait_read(pe, "kv", 2 * b + 1)
                dst = take("state", b)
                for g in range(FB):
                    for i in range(2):
                        ins = mm(dst[:, g * VW:(g + 1) * VW], kp[:, (2 * b + i) % HT, g * P:(g + 1) * P], vx[:, (2 * b + i) % HT, g, :],
                                 start=(i == 0), stop=(i == 1))
                done(ins, "state", b)

            def z_sum(b):
                pe.wait_ge(s["q"], FB * (b // BPH) + FB)
                wait_read(pe, "state", b)
                dst = take("z", b)
                for i in range(2):
                    for g in range(FB):
                        at = (FB * i + g) * HPB
                        ins = mm(dst[:, at:at + HPB], qT[:, g, (2 * b + i) * P:(2 * b + i + 1) * P], ks[:, b, g, :],
                                 start=True, stop=True)
                done(ins, "z", b)

            def attend(b):
                dst = take("num", b)
                for g in range(FB):
                    ins = mm(dst[:, g * SEQ:(g + 1) * SEQ], bd[:, b, g, :], qT[:, g, b * SEQ:(b + 1) * SEQ],
                             start=True, stop=True)
                done(ins, "num", b)

            def spread_z(b):
                pe.wait_ge(s["z_spread"], b + 1)
                dst = take("rz", b)
                for g in range(FB):
                    for i in range(2):
                        ins = nc.tensor.transpose(dst[:, g * SEQ + i * P:g * SEQ + (i + 1) * P],
                                                  zr[:, b % 2, (FB * i + g) * P:(FB * i + g + 1) * P], ident)
                done(ins, "rz", b)

            def o_proj(p):
                wait_read(pe, "num", p)
                dst = take("out", p)
                for i in range(2):
                    for k in range(FB):
                        ins = mm(dst[:, i * HID:(i + 1) * HID], qT[:, k, (2 * p + i) * P:(2 * p + i + 1) * P], wo[:, k, :],
                                 start=(k == 0), stop=(k == FB - 1))
                done(ins, "out", p)

            def w_down(n):
                dst = take("wd", n)
                for part in range(2):
                    ins = mm(dst[:, :], had_d[:, :], dpre[:, part, 2 * n:2 * n + 2, :].rearrange("p n o -> p (n o)"),
                             start=(part == 0), stop=(part == 1))
                done(ins, "wd", n)

            def x2_turn(h):
                pe.wait_ge(s["x2"], HT * (h + 1))
                turn("x2T", h, xs[:, h * HT:(h + 1) * HT, :])

            def x3_turn(h):
                pe.wait_ge(s["xn3"], HT * (h + 1))
                turn("x3T", h, xn)

            def hadamard_x(h):
                for f in range(FB):
                    wait_read(pe, "x3T", h, f)
                for f in range(FB):
                    dst = take("xh", h, f)
                    for k in range(FB):
                        for part in range(2):
                            ins = mm(dst[:, :], (had_m if f and k else had_u)[:, :], xs3[:, part, k, :],
                                     start=(k == 0 and part == 0), stop=(k == FB - 1 and part == 1))
                    done(ins, "xh", h, f)

            PARTS = ((1, 0), (0, 1), (0, 0))

            def ffn_up(h, j):
                for name, at in (("gate", INTER), ("up", 0)):
                    dst = take(name, h, j)
                    for k in range(FB):
                        for i, (a, b) in enumerate(PARTS):
                            ins = mm(dst[:, :], wug[:, a, k, at + j * P:at + (j + 1) * P], xh[:, b, h, k, :],
                                     start=(k == 0 and i == 0), stop=(k == FB - 1 and i == 2))
                    done(ins, name, h, j)

            def ffn_down(h, j):
                n = JB * h + j
                pe.wait_ge(s["h_lo"], n + 1)
                for o in range(FB):
                    if j == 0:
                        take("y", h, o)
                    for i, (a, b) in enumerate(PARTS):
                        ins = mm(B("y", h, o)[:, :], wdh[:, a, j, o * P:(o + 1) * P], hsp[:, b, n % HR, :],
                                 start=(j == 0 and i == 0), stop=(j == JB - 1 and i == 2))
                    if j == JB - 1:
                        done(ins, "y", h, o)
                if j < JB - 1:
                    ins.then_inc(s["h_used"], 1)

            pe.wait_ge(s["junk_ready"], 1)
            for _ in range(WARM):
                mm(bank[BANKS - 1][:, :], junk[:, 0:P], junk[:, :], start=True, stop=True)
            pe.wait_ge(ld["cst"], 16)
            norm1(0)
            pe.wait_ge(ld["ctx"], 16)
            pe.wait_ge(ld["wx"], 16)
            project("qp", 0)
            project("kp", 0)
            pe.wait_ge(s["w_lo"], 1)
            q_proj(0)
            pe.wait_ge(s["w_lo"], 2)
            for t in range(HT):
                kv_proj(t)
            norm1(1)
            project("qp", 1)
            project("kp", 1)
            pe.wait_ge(s["ones_ready"], 1)
            state(0)
            state(1)
            q_proj(1)
            z_sum(0)
            z_sum(1)
            attend(0)
            attend(1)
            scores(0)
            kv_proj(4)
            kv_proj(5)
            spread_z(0)
            spread_z(1)
            kv_proj(6)
            kv_proj(7)
            scores(1)
            pe.wait_ge(ld["wo"], 16)
            o_proj(0)
            o_proj(1)
            state(2)
            state(3)
            scores(2)
            scores(3)
            z_sum(2)
            z_sum(3)
            attend(2)
            attend(3)
            pe.wait_ge(s["pre_lo"], 2)
            pe.wait_ge(s["had_ready"], 3)
            w_down(0)
            w_down(1)
            w_down(2)
            w_down(3)
            spread_z(2)
            spread_z(3)
            o_proj(2)
            o_proj(3)
            x2_turn(0)
            x3_turn(0)
            hadamard_x(0)
            pe.wait_ge(s["ug_lo_v"], 2)
            for f in range(FB):
                wait_read(pe, "xh", 0, f)
            for h in range(HALVES):
                if h:
                    for f in range(FB):
                        wait_read(pe, "xh", 1, f)
                for j in range(JB):
                    if h == 0 and j == JB // 2:
                        pe.wait_ge(s["ug_lo_p"], 2)
                    ffn_up(h, j)
                    if j == 2 and h == 0:
                        for n in range(4):
                            wait_read(pe, "wd", n)
                    if j >= 2:
                        ffn_down(h, j - 2)
                    if h == 0 and j in TAIL_AT:
                        {"x2T": x2_turn, "x3T": x3_turn, "xh": hadamard_x}[TAIL_AT[j]](1)
                ffn_down(h, JB - 2)
                ffn_down(h, JB - 1)


def kernel(**inputs):
    import concourse.bacc as _bacc
    from concourse.bass_utils import run_bass_kernel_spmd as _run

    a = {k: np.asarray(v) for k, v in inputs.items()}

    def blocks(w):
        return w.reshape(-1, P, w.shape[-1]).transpose(1, 0, 2)

    def columns(w):
        return w.reshape(-1, P).T

    zero = np.zeros((P - CTX, 2), np.float32)
    eye, ones = np.eye(P, dtype=np.float32), np.ones((HD, HD), np.float32)
    arrays = {
        "x": blocks(a["x"].reshape(TOK, HID)),
        "ctx_t": a["ctx_512"].reshape(TOK, CTX).T,
        "w_qkv": blocks(np.concatenate([a["L0_attn_q_w"], a["L0_attn_k_w"], a["L0_attn_v_w"]]).T),
        "w_o": blocks(a["L0_attn_o_w"].T),
        "w_x": np.concatenate([a["L0_xattn_Wq"], a["L0_xattn_Wk"]]).T,
        "w_ug": blocks(np.concatenate([a["L0_ffn_W_up"], a["L0_ffn_W_gate"]]).T),
        "w_d": blocks(a["L0_ffn_W_down"].T),
        "vec": np.concatenate([columns(a[n]) for n in ("L0_attn_q_b", "L0_ffn_SU_ug", "L0_ffn_SU_dp",
                                                       "L0_ffn_Wscale_ug", "L0_ffn_Wscale_dp")]
                              + [np.concatenate([np.stack([a["L0_xattn_bq"], a["L0_xattn_bk"]], 1), zero])], 1),
        "row": np.concatenate([a[n] for n in ("L0_attn_k_b", "L0_attn_v_b", "L0_attn_o_b")]),
        "mask_ss": blocks(a["mask_SxS2_bk1"]),
        "mask_key": a["mask_BxS2_bf0"],
        "const": np.concatenate([eye, hadamard(P), np.tile(np.kron(np.eye(P // HD, dtype=np.float32), ones), (1, FB)),
                                 np.tile(np.kron(np.eye(P // HD, dtype=np.float32), ones[:, 0:1]), (1, FB))], 1),
    }
    nc = _bacc.Bacc("TRN2", target_bir_lowering=False, num_devices=1)
    sent, args = {}, []
    for name, arr in arrays.items():
        arr = np.ascontiguousarray(arr)
        sent[f"in_{name}"] = arr
        args.append(nc.dram_tensor(f"in_{name}", arr.shape, mybir.dt.from_np(arr.dtype), kind="ExternalInput").ap())
    args.append(nc.dram_tensor("out_0", (P, FB, TOK), F32, kind="ExternalOutput").ap())
    decoder_kernel(nc, *args)
    got = _run(nc, [sent], core_ids=[0]).results[0]["out_0"]
    return np.ascontiguousarray(got.transpose(2, 1, 0)).reshape(BATCH, SEQ, HID)
```

```python
import concourse.bass as bass
import numpy as np
from concourse import mybir
from contextlib import ExitStack

F32 = mybir.dt.float32
F32R = mybir.dt.float32r
BF16 = mybir.dt.bfloat16
U8 = mybir.dt.uint8
ALU = mybir.AluOpType
ACT = mybir.ActivationFunctionType

P = 128
BATCH, SEQ, HID = 4, 256, 256
CTX = 64
CTX1 = CTX + 1
HD = 16
INTER = 1024
TOK = BATCH * SEQ
TILES = TOK // P
HALVES = 2
HT = TILES // HALVES
HTOK = TOK // HALVES
ST = SEQ // P
BPH = BATCH // HALVES
FB = HID // P
JB = INTER // P
WDP = 2
WDB = JB // WDP
STAGES = (JB - 1).bit_length()
LN_EPS = 1e-5
Z_EPS = 1e-6
BANKS = 8
WARM, WARM_MORE = 8, 7
MASKED = 3.0e35
HIGHEST = 1.0e20

V_QB, V_SUG, V_SUD, V_WSUG, V_WSD, V_COLS = 0, 2, 4, 12, 28, 30
UG_ORDER = (0, 2, 1, 3)
PASSES = ((0, 1, 0), (0, 0, 0), (1, 1, 0), (1, 0, 0), (0, 0, 1), (1, 0, 1))
KV_PASSES = ((0, 0, 0), (1, 0, 0), (0, 0, 1), (1, 0, 1), (0, 1, 0), (1, 1, 0))

LAG = 3
HR = LAG + 1
ASIDE = {6: ("x3T", 1), 7: ("xh", 1), 8: ("x2T", 0), 9: ("x2T", 1)}

PIECES = ((0, 0, 0, 0, HTOK), (0, 1, 0, 0, HTOK), (1, 0, 0, 0, HTOK), (1, 1, 0, 0, HTOK // 2), (1, 1, 1, HTOK // 2, HTOK))


def hadamard(n):
    h = np.ones((1, 1), np.float32)
    while h.shape[0] < n:
        h = np.block([[h, h], [h, -h]])
    return h.astype(np.float32)


def schedule():
    order = [(("xnT", 0, 0), 0), (("xnT", 0, 1), 1), (("mx",), 3), (("u", 0), 2), (("q", 0, 0), 4), (("q", 0, 1), 5),
             (("kv", 0), 6), (("kv", 1), 7), (("kv", 2), 0), (("kv", 3), 1), (("xnT", 1, 0), 4), (("xnT", 1, 1), 5),
             (("u", 1), 3), (("state", 0), 6), (("state", 1), 7), (("q", 1, 0), 0), (("num", 0), 1),
             (("num", 1), 2), (("num", 2), 4), (("num", 3), 5), (("q", 1, 1), 3), (("attnT", 0), 6), (("attnT", 1), 7),
             (("kv", 4), 0), (("out", 0), 1), (("out", 1), 2), (("kv", 5), 4), (("score", 0), 5), (("score", 1), 3),
             (("kv", 6), 6), (("kv", 7), 7), (("state", 2), 0), (("score", 2), 1), (("wd", 0), 6), (("score", 3), 2),
             (("num", 4), 5), (("num", 5), 3), (("state", 3), 4), (("num", 6), 0), (("num", 7), 4), (("attnT", 2), 1),
             (("wd", 1), 7), (("out", 2), 5), (("attnT", 3), 2), (("x3T", 0, 0), 1), (("x3T", 0, 1), 2), (("out", 3), 3),
             (("xh", 0, 0), 0), (("xh", 0, 1), 4), (("wd", 2), 5), (("wd", 3), 3)]
    for h in range(HALVES):
        for j in range(JB):
            n = JB * h + j
            pair = (6, 7) if n == 2 else ((1, 2), (0, 4))[n % 2]
            order += [(("gate", h, j), pair[0]), (("up", h, j), pair[1])]
            if j == LAG:
                order += [(("y", h, o, 0), (5, 3)[o]) for o in range(FB)]
                order += [(("y", h, FB - 1, 1), 7)] if h == HALVES - 1 else []
            if n in ASIDE:
                order += [((*ASIDE[n], f), 6 + f) for f in range(FB)]
    return order


def decoder_kernel(nc, x, ctx_t, w_qkv, w_o, w_x, w_ug, w_d, vec, row, mask_ss, mask_key, const, out):
    order = schedule()
    bank_of, turn_of, uses = {}, {}, [0] * BANKS
    for group, bank in order:
        bank_of[group], turn_of[group] = bank, uses[bank]
        uses[bank] += 1

    stack = ExitStack()
    with stack:
        def sb(name, shape, dt=F32):
            return stack.enter_context(nc.sbuf_tensor(name, shape, dt))

        def sem(name):
            return stack.enter_context(nc.semaphore(name))

        xs = sb("x_res", [P, TILES, HID])
        wqkv = sb("wqkv", [P, 2, FB, 3 * HID], F32R)
        wo = sb("wo", [P, FB, HID])
        wx = sb("wx", [CTX, 2 * CTX1])
        ctxT = sb("ctxT", [CTX1, TOK])
        vecs = sb("vecs", [P, V_COLS])
        rows = sb("rows", [P, 3 * HID])
        HPB = P // HD
        cst = sb("cst", [P, 2 * P + HID + FB * HPB])
        ident, had, same_head = cst[:, 0:P], cst[:, P:2 * P], cst[:, 2 * P:2 * P + HID]
        head_of = cst[:, 2 * P + HID:]
        mss = sb("mss", [P, ST, SEQ], U8)
        mkey = sb("mkey", [P, BATCH, SEQ], U8)
        bss = sb("bss", [P, ST, SEQ], BF16)
        bkey = sb("bkey", [P, BATCH, SEQ], BF16)
        mbias = sb("mbias", [P, TILES, SEQ], BF16)
        junk = mbias[:, 0:2, :].rearrange("p t s -> p (t s)")
        had_u = sb("had_u", [P, P], F32R)
        had_m = sb("had_m", [P, P], F32R)
        had_d = sb("had_d", [P, P], F32R)
        st = sb("st", [P, TILES, 6])
        mv = sb("mv", [P, 3, TILES, 2])
        veps = sb("veps", [P, 3, TILES])
        rstd = sb("rstd", [P, 3, TILES])
        mhalf = sb("mhalf", [P, TILES])
        exp_first = sb("exp_first", [P, TILES])
        xn = sb("xn", [P, HT, HID])
        eq = sb("eq", [P, 2, HTOK])
        qT = sb("qT", [P, FB, TOK])
        kt = sb("kt", [P, 2, HID])
        ek = sb("ek", [P, 2, HID])
        rk = sb("rk", [P, 2, HID])
        kp = sb("kp", [P, HT, HID])
        VW = P + 2
        vx = sb("vx", [P, HT, FB, VW])
        SW = P + HPB
        kvs = sb("kvs", [P, BATCH, FB, SW])
        ze = sb("ze", [P, TILES, FB * HPB])
        zi = sb("zi", [P, TILES, FB * HPB])
        at = sb("at", [P, 2, 2, HID])
        mx = sb("mx", [CTX1, CTX1])
        ux = sb("ux", [CTX1, TOK])
        score = sb("score", [P, TILES, SEQ])
        low = sb("low", [P, TILES])
        row_sum = sb("row_sum", [P, TILES])
        rsum = sb("rsum", [P, TILES])
        stage = sb("stage", [P, 2, FB, 512])
        wug = sb("wug", [P, 2, FB, 2 * INTER], F32R)
        wd_raw = sb("wd_raw", [P, JB, HID])
        wd_alt = sb("wd_alt", [P, JB, HID])
        dpre = sb("dpre", [P, 2, JB, HID], F32R)
        wdh = sb("wdh", [P, 2, JB, HID], F32R)
        xs3 = sb("xs3", [P, 2, FB, HTOK], F32R)
        xh = sb("xh", [P, 2, HALVES, FB, HTOK], F32R)
        sg = eq
        wd_a, wd_b = wd_raw[:, :, :], wd_alt[:, :, :]
        qkv_raw = stage[:, :, :, :].rearrange("p a f n -> p (a f n)")[:, 0:FB * 3 * HID]\
            .rearrange("p (f n) -> p f n", f=FB)
        hsp = dpre[:, :, :, :].rearrange("p l (n r) o -> p l n (r o)", n=HR)
        x2T = score[:, :, :].rearrange("p (h f a) s -> p h f (a s)", h=HALVES, f=FB)

        bank = [stack.enter_context(nc.psum_tensor(f"bank{i}", [P, 512], F32)) for i in range(BANKS)]
        full = [sem(f"bank_full{i}") for i in range(BANKS)]
        read = [sem(f"bank_read{i}") for i in range(BANKS)]

        def B(*group):
            return bank[bank_of[group]]

        def wait_full(eng, *group):
            eng.wait_ge(full[bank_of[group]], turn_of[group] + 1)

        def read_of(*group):
            return read[bank_of[group]]

        def wait_read(eng, *group):
            eng.wait_ge(read[bank_of[group]], turn_of[group] + 1)

        loads = ("x0 x0_rest x1 ctx wx wq wkv wo vec row ident cst mss mkey ug0 ug1 ug2 ug3 wd "
                 "out0 out1 out2 out3 out4").split()
        ld = {n: sem("ld_" + n) for n in loads}
        names = ("mhalf_ready junk_ready ones_ready had_ready mask_value mbias "
                 "stats1 aggr1 eps1 rstd1 xn1 stats2 aggr2 eps2 rstd2 stats3 aggr3 eps3 rstd3 xn3 "
                 "w_hi wq_lo wkv_lo ug_hi ug_lo_v ug_lo_p fly pre_hi pre_lo wd_hi "
                 "xnT_hi eq q kt nk rk kp z_eps z_inv xb "
                 "sx logit prob rsum x2 "
                 "xs_hi xh_hi h_hi h_lo h_last h_used y").split()
        s = {n: sem("s_" + n) for n in names}

        block = stack.enter_context(nc.Block())

        def h_slot_free(eng, n):
            m = n - HR
            if m >= 0 and m % JB == JB - 1:
                wait_full(eng, "y", m // JB, FB - 1, 0)
            elif m >= 0:
                eng.wait_ge(s["h_used"], m + 1 - m // JB)

        @block.sync
        def _(sp):
            sp.dma_start(xs[:, 0:HT // 2, :], x[:, 0:HT // 2, :]).then_inc(ld["x0"], 16)
            sp.dma_start(xs[:, HT // 2:HT, :], x[:, HT // 2:HT, :]).then_inc(ld["x0_rest"], 16)
            sp.dma_start(cst[:, 0:P], const[:, 0:P]).then_inc(ld["ident"], 16)
            sp.dma_start(qkv_raw[:, :, HID:3 * HID], w_qkv[:, :, HID:3 * HID]).then_inc(ld["wkv"], 16)
            sp.dma_start(xs[:, HT:TILES, :], x[:, HT:TILES, :]).then_inc(ld["x1"], 16)
            sp.dma_start(wd_a, w_d).then_inc(ld["wd"], 16)
            sp.dma_start(rows[:, :], row.partition_broadcast(P)).then_inc(ld["row"], 16)
            sp.dma_start(mss[:, :, :], mask_ss).then_inc(ld["mss"], 16)
            sp.dma_start(mkey[:, :, :], mask_key.partition_broadcast(P)).then_inc(ld["mkey"], 16)
            sp.dma_start(wo[:, :, :], w_o).then_inc(ld["wo"], 16)
            for n, c in enumerate(UG_ORDER):
                if n < 2:
                    sp.wait_ge(s["w_hi"], 2)
                    sp.wait_ge(s["wq_lo"], 1)
                    sp.wait_ge(s["wkv_lo"], 1)
                else:
                    sp.wait_ge(s["ug_hi"], n - 1)
                    sp.wait_ge(s["ug_lo_v" if n == 2 else "ug_lo_p"], 1)
                sp.dma_start(stage[:, n % 2, :, :], w_ug[:, :, c * 512:(c + 1) * 512]).then_inc(ld[f"ug{n}"], 16)
            for n, (h, o, _, a, z) in enumerate(PIECES):
                sp.wait_ge(s["y"], n + 1)
                sp.dma_start(out[:, o, h * HTOK + a:h * HTOK + z], x2T[:, h, o, a:z]).then_inc(ld[f"out{n}"], 16)
            for n in range(len(PIECES)):
                sp.wait_ge(ld[f"out{n}"], 16)

        @block.gpsimd
        def _(pool):
            g = nc.gpsimd
            g.memset(mhalf[:, :], -0.5).then_inc(s["mhalf_ready"], 1)
            g.memset(junk[:, :], 0.0).then_inc(s["junk_ready"], 1)
            g.memset(vx[:, :, :, P:VW], 1.0).then_inc(s["ones_ready"], 1)
            pool.wait_ge(s["mhalf_ready"], 1)

            def rstd_of(n, a, z):
                pool.wait_ge(s[f"aggr{n}"], z)
                g.tensor_scalar(veps[:, n - 1, a:z], mv[:, n - 1, a:z, 1], LN_EPS, None, ALU.add).then_inc(s[f"eps{n}"], z - a)
                pool.wait_ge(s[f"eps{n}"], z)
                g.tensor_tensor(rstd[:, n - 1, a:z], veps[:, n - 1, a:z], mhalf[:, a:z], ALU.pow).then_inc(s[f"rstd{n}"], z - a)

            def add_ob(t):
                pool.wait_ge(s["xn1"], t + 1)
                g.tensor_tensor(xs[:, t, :], xs[:, t, :], rows[:, 2 * HID:3 * HID], ALU.add).then_inc(s["xb"], 1)

            def sum_k(t):
                pool.wait_ge(s["rk"], t + 1)
                g.tensor_tensor(kp[:, t % HT, :], ek[:, t % 2, :], rk[:, t % 2, :], ALU.add).then_inc(s["kp"], 1)

            def mask_bias():
                pool.wait_ge(s["mask_value"], 2)
                for i in range(ST):
                    g.tensor_tensor(mbias[:, i:TILES:ST, :], bss[:, i:i + 1, :].to_broadcast([P, BATCH, SEQ]),
                                    bkey[:, :, :], ALU.add).then_inc(s["mbias"], 1)

            def wkv_lo():
                pool.wait_ge(s["w_hi"], 2)
                g.tensor_tensor(wqkv[:, 1, :, HID:3 * HID], qkv_raw[:, :, HID:3 * HID],
                                wqkv[:, 0, :, HID:3 * HID].bitcast(F32), ALU.subtract).then_inc(s["wkv_lo"], 1)

            def ug_lo(n):
                c = UG_ORDER[n]
                pool.wait_ge(s["ug_hi"], n + 1)
                g.tensor_tensor(wug[:, 1, :, c * 512:(c + 1) * 512], stage[:, n % 2, :, :],
                                wug[:, 0, :, c * 512:(c + 1) * 512].bitcast(F32), ALU.subtract).then_inc(s["ug_lo_p"], 1)

            def pre_lo(n):
                part = slice(n * JB // 2, (n + 1) * JB // 2)
                pool.wait_ge(s["pre_hi"], n + 1)
                g.tensor_tensor(dpre[:, 1, part, :], wd_b[:, part, :], dpre[:, 0, part, :].bitcast(F32),
                                ALU.subtract).then_inc(s["pre_lo"], 1)

            def butterfly(stage_no):
                if stage_no:
                    pool.wait_ge(s["fly"], 2 * stage_no)
                src, dst = ((wd_a, wd_b), (wd_b, wd_a))[stage_no % 2]
                src, dst = (w.rearrange("p (u two v) o -> p u two (v o)", two=2, v=JB >> (stage_no + 1)) for w in (src, dst))
                g.tensor_tensor(dst[:, :, 0, :], src[:, :, 0, :], src[:, :, 1, :], ALU.add).then_inc(s["fly"], 1)
                g.tensor_tensor(dst[:, :, 1, :], src[:, :, 0, :], src[:, :, 1, :], ALU.subtract).then_inc(s["fly"], 1)

            rstd_of(1, 0, HT // 2)
            rstd_of(1, HT // 2, HT)
            wkv_lo()
            rstd_of(1, HT, TILES)
            pool.wait_ge(ld["wd"], 16)
            for stage_no in range(STAGES):
                butterfly(stage_no)
            pool.wait_ge(ld["row"], 16)
            for t in range(HT):
                add_ob(t)
            mask_bias()
            sum_k(HT)
            sum_k(HT + 1)
            rstd_of(2, 0, HT)
            pre_lo(0)
            sum_k(HT + 2)
            sum_k(HT + 3)
            pre_lo(1)
            for t in range(HT, TILES):
                add_ob(t)
            rstd_of(3, 0, HT)
            ug_lo(1)
            ug_lo(2)
            for n in range(HALVES * JB - 1):
                pool.wait_ge(s["h_hi"], n + 1)
                h_slot_free(pool, n)
                g.tensor_tensor(hsp[:, 1, n % HR, :], sg[:, n % 2, :], hsp[:, 0, n % HR, :].bitcast(F32),
                                ALU.subtract).then_inc(s["h_lo"], 1)
                if n == 0:
                    rstd_of(2, HT, TILES)
                    ug_lo(3)
                if n == 2:
                    rstd_of(3, HT, TILES)

        @block.scalar
        def _(act):
            a = nc.scalar
            act.dma_start(wx[:, :], w_x).then_inc(ld["wx"], 16)
            act.dma_start(qkv_raw[:, :, 0:HID], w_qkv[:, :, 0:HID]).then_inc(ld["wq"], 16)
            act.dma_start(ctxT[:, :], ctx_t).then_inc(ld["ctx"], 16)
            act.dma_start(vecs[:, :], vec).then_inc(ld["vec"], 16)
            act.dma_start(cst[:, P:], const[:, P:]).then_inc(ld["cst"], 16)
            act.wait_ge(s["mhalf_ready"], 1)
            a.activation(exp_first[:, :], mhalf[:, :], ACT.Exp)


            def mx_evac():
                wait_full(act, "mx")
                a.copy(mx[:, :], B("mx")[0:CTX1, 0:CTX1]).then_inc(read_of("mx"), 1)

            def u_evac(c):
                wait_full(act, "u", c)
                a.copy(ux[:, c * 512:(c + 1) * 512], B("u", c)[0:CTX1, :]).then_inc(read_of("u", c), 1)

            def w_hi(n):
                act.wait_ge(ld[("wq", "wkv")[n]], 16)
                cols = (slice(0, HID), slice(HID, 3 * HID))[n]
                a.copy(wqkv[:, 0, :, cols], qkv_raw[:, :, cols]).then_inc(s["w_hi"], 1)

            def xnT_hi(h):
                for f in range(FB):
                    wait_full(act, "xnT", h, f)
                    a.copy(xs3[:, 0, f, :], B("xnT", h, f)[:, :]).then_inc(s["xnT_hi"], 1)

            def scores(b):
                wait_full(act, "score", b)
                a.mul(score[:, 2 * b:2 * b + 2, :].rearrange("p t s -> p (t s)"), B("score", b)[:, :],
                      -float(CTX) ** -0.5).then_inc(read_of("score", b), 1)

            def exp_q(h, m):
                n = FB * h + m
                wait_full(act, "q", h, m)
                if n >= 2:
                    act.wait_ge(s["q"], n - 1)
                a.activation(eq[:, n % 2, :], B("q", h, m)[:, :], ACT.Exp,
                             bias=vecs[:, V_QB + m:V_QB + m + 1]).then_inc(s["eq"], 1)

            def exp_k(t):
                act.wait_ge(s["kt"], t + 1)
                if t >= 2:
                    act.wait_ge(s["kp"], t - 1)
                a.activation(ek[:, t % 2, :], kt[:, t % 2, :], ACT.Exp)
                a.activation(rk[:, t % 2, :], kt[:, t % 2, :], ACT.Relu).then_inc(s["rk"], 1)

            def attnT_evac(b):
                wait_full(act, "attnT", b)
                a.copy(qT[:, :, b * SEQ:(b + 1) * SEQ], B("attnT", b)[:, :].rearrange("p (g s) -> p g s", g=FB))\
                    .then_inc(read_of("attnT", b), 1)

            def elu_k_parts(t):
                act.wait_ge(s["kt"], t + 1)
                act.wait_ge(s["kp"], t - 1)
                a.activation(ek[:, t % 2, :], kt[:, t % 2, :], ACT.Relu, scale=-1.0).then_inc(s["nk"], 1)
                a.activation(rk[:, t % 2, :], kt[:, t % 2, :], ACT.Relu)
                act.wait_ge(s["nk"], t - HT + 1)
                a.activation(ek[:, t % 2, :], ek[:, t % 2, :], ACT.Exp, scale=-1.0).then_inc(s["rk"], 1)

            def mask_value():
                act.wait_ge(ld["mss"], 16)
                a.mul(bss[:, :, :], mss[:, :, :], MASKED).then_inc(s["mask_value"], 1)
                act.wait_ge(ld["mkey"], 16)
                a.mul(bkey[:, :, :], mkey[:, :, :], MASKED).then_inc(s["mask_value"], 1)

            def wd_hi(n):
                wait_full(act, "wd", n)
                for i in range(WDP):
                    j = WDP * n + i
                    a.activation(wdh[:, 0, j, :], B("wd", n)[:, i * HID:(i + 1) * HID], ACT.Copy,
                                 scale=vecs[:, V_SUD + j:V_SUD + j + 1]).then_inc(s["wd_hi"], 1)

            def pre_hi(n):
                part = slice(n * JB // 2, (n + 1) * JB // 2)
                act.wait_ge(s["fly"], 2 * STAGES)
                a.copy(dpre[:, 0, part, :], wd_b[:, part, :]).then_inc(s["pre_hi"], 1)

            def ug_hi(n):
                c = UG_ORDER[n]
                act.wait_ge(ld[f"ug{n}"], 16)
                a.copy(wug[:, 0, :, c * 512:(c + 1) * 512], stage[:, n % 2, :, :]).then_inc(s["ug_hi"], 1)

            def prob(t):
                act.wait_ge(s["logit"], t + 1)
                a.activation(score[:, t, :], score[:, t, :], ACT.Exp, bias=low[:, t:t + 1], scale=-1.0,
                             accum_out=row_sum[:, t:t + 1]).then_inc(s["prob"], 1)

            def x2T_evac(h):
                for f in range(FB):
                    wait_full(act, "x2T", h, f)
                    a.copy(x2T[:, h, f, :], B("x2T", h, f)[:, :]).then_inc(read_of("x2T", h, f), 1)

            def x3T_hi(h):
                for f in range(FB):
                    wait_full(act, "x3T", h, f)
                    if h:
                        wait_full(act, "xh", 0, 1)
                    a.activation(xs3[:, 0, f, :], B("x3T", h, f)[:, :], ACT.Copy,
                                 scale=vecs[:, V_SUG + f:V_SUG + f + 1]).then_inc(s["xs_hi"], 1)

            def xh_hi(h):
                for f in range(FB):
                    wait_full(act, "xh", h, f)
                    a.copy(xh[:, 0, h, f, :], B("xh", h, f)[:, :]).then_inc(s["xh_hi"], 1)

            mx_evac()
            w_hi(0)
            xnT_hi(0)
            w_hi(1)
            u_evac(0)
            act.wait_ge(ld["vec"], 16)
            exp_q(0, 0)
            exp_q(0, 1)
            act.wait_ge(ld["cst"], 16)
            for m, scale in ((had_u, HID ** -0.5), (had_m, -(HID ** -0.5)), (had_d, INTER ** -0.5)):
                a.mul(m[:, :], had, scale).then_inc(s["had_ready"], 1)
            for t in range(HT):
                exp_k(t)
            xnT_hi(1)
            u_evac(1)
            mask_value()
            exp_q(1, 0)
            ug_hi(0)
            exp_q(1, 1)
            attnT_evac(0)
            attnT_evac(1)
            ug_hi(1)
            elu_k_parts(HT)
            pre_hi(0)
            pre_hi(1)
            elu_k_parts(HT + 1)
            scores(0)
            scores(1)
            ug_hi(2)
            elu_k_parts(HT + 2)
            elu_k_parts(HT + 3)
            for t in range(HT):
                prob(t)
            scores(2)
            scores(3)
            wd_hi(0)
            attnT_evac(2)
            wd_hi(1)
            attnT_evac(3)
            x3T_hi(0)
            xh_hi(0)
            wd_hi(2)
            wd_hi(3)
            for h in range(HALVES):
                for j in range(JB):
                    n = JB * h + j
                    if n >= 2:
                        act.wait_ge(s["h_lo"], n - 1)
                    wait_full(act, "gate", h, j)
                    a.activation(sg[:, n % 2, :], B("gate", h, j)[:, :], ACT.Silu,
                                 scale=vecs[:, V_WSUG + JB + j:V_WSUG + JB + j + 1]).then_inc(read_of("gate", h, j), 1)
                    if n == 2:
                        for t in range(HT, TILES):
                            prob(t)
                    wait_read(act, "up", h, j)
                    h_slot_free(act, n)
                    a.copy(hsp[:, 0, n % HR, :], sg[:, n % 2, :]).then_inc(s["h_hi"], 1)
                    if n == 0:
                        ug_hi(3)
                    if n in ASIDE:
                        step, half = ASIDE[n]
                        {"x2T": x2T_evac, "x3T": x3T_hi, "xh": xh_hi}[step](half)

        @block.vector
        def _(dve):
            v = nc.vector

            def norm_stats(n, t):
                if n == 2:
                    wait_read(dve, "out", t // 2)
                v.bn_stats(st[:, t, :], xs[:, t, :]).then_inc(s[f"stats{n}"], 1)

            def norm_aggr(n, t):
                dve.wait_ge(s[f"stats{n}"], t + 1)
                v.bn_aggr(mv[:, n - 1, t, :], st[:, t, :]).then_inc(s[f"aggr{n}"], 1)

            def normalise(n, t):
                dve.wait_ge(s[f"rstd{n}"], t + 1)
                if n == 1:
                    dve.wait_ge(s["aggr1"], t + 1)
                v.tensor_scalar(xn[:, t % HT, :], xs[:, t, :], mv[:, n - 1, t, 0:1], rstd[:, n - 1, t:t + 1],
                                ALU.subtract, ALU.mult).then_inc(s[f"xn{n}"], 1)

            def ln1_stats(a, z, load):
                dve.wait_ge(ld[load], 16)
                for t in range(a, z):
                    norm_stats(1, t)
                for t in range(a, z):
                    norm_aggr(1, t)

            def ln1(h):
                for t in range(h * HT, (h + 1) * HT):
                    normalise(1, t)

            def wq_lo():
                dve.wait_ge(s["w_hi"], 1)
                v.tensor_tensor(wqkv[:, 1, :, 0:HID], qkv_raw[:, :, 0:HID], wqkv[:, 0, :, 0:HID].bitcast(F32),
                                ALU.subtract).then_inc(s["wq_lo"], 1)

            def ug_lo(n):
                c = UG_ORDER[n]
                dve.wait_ge(s["ug_hi"], n + 1)
                v.tensor_tensor(wug[:, 1, :, c * 512:(c + 1) * 512], stage[:, n % 2, :, :],
                                wug[:, 0, :, c * 512:(c + 1) * 512].bitcast(F32), ALU.subtract).then_inc(s["ug_lo_v"], 1)

            def xnT_lo(h):
                for f in range(FB):
                    dve.wait_ge(s["xnT_hi"], FB * h + f + 1)
                    v.tensor_tensor(xs3[:, 1, f, :], B("xnT", h, f)[:, :], xs3[:, 0, f, :].bitcast(F32),
                                    ALU.subtract).then_inc(read_of("xnT", h, f), 1)

            def elu_q(h, m):
                n = FB * h + m
                dve.wait_ge(s["eq"], n + 1)
                into = qT[:, m, h * HTOK:(h + 1) * HTOK]
                v.tensor_scalar(into, B("q", h, m)[:, :], vecs[:, V_QB + m:V_QB + m + 1], 0.0,
                                ALU.add, ALU.max).then_inc(read_of("q", h, m), 1)
                wait_read(dve, "q", h, m)
                v.scalar_tensor_tensor(into, eq[:, n % 2, :], 1.0, into, ALU.min, ALU.add).then_inc(s["q"], 1)

            def kv(t):
                wait_full(dve, "kv", t)
                if t >= 2:
                    dve.wait_ge(s["kp"], t - 1)
                v.tensor_tensor(kt[:, t % 2, :], B("kv", t)[:, 0:HID], rows[:, 0:HID], ALU.add).then_inc(s["kt"], 1)
                v.tensor_tensor(vx[:, t % HT, :, 0:P], B("kv", t)[:, HID:2 * HID].rearrange("p (g e) -> p g e", g=FB),
                                rows[:, HID:2 * HID].rearrange("p (g e) -> p g e", g=FB),
                                ALU.add).then_inc(read_of("kv", t), 1)

            def elu_k(t):
                dve.wait_ge(s["rk"], t + 1)
                v.scalar_tensor_tensor(kp[:, t % HT, :], ek[:, t % 2, :], 1.0, rk[:, t % 2, :],
                                       ALU.min, ALU.add).then_inc(s["kp"], 1)

            def diagonal(b):
                wait_full(dve, "state", b)
                got = B("state", b)[:, 0:FB * VW].rearrange("p (g e) -> p g e", g=FB)
                v.tensor_tensor(kvs[:, b, :, 0:P], got[:, :, 0:P], same_head.rearrange("p (g e) -> p g e", g=FB), ALU.mult)
                v.tensor_tensor(kvs[:, b, :, P:SW], got[:, :, P:P + 1].to_broadcast([P, FB, HPB]),
                                head_of.rearrange("p (g h) -> p g h", g=FB), ALU.mult).then_inc(read_of("state", b), 1)

            def num_of(t):
                return B("num", t)[:, 0:FB * SW].rearrange("p (g e) -> p g e", g=FB)

            def z_inverse(b):
                two = slice(2 * b, 2 * b + 2)
                for t in range(2 * b, 2 * b + 2):
                    wait_full(dve, "num", t)
                    v.tensor_scalar(ze[:, t, :].rearrange("p (g h) -> p g h", g=FB), num_of(t)[:, :, P:SW], Z_EPS, None,
                                    ALU.add).then_inc(s["z_eps"], 1)
                dve.wait_ge(s["z_eps"], 2 * b + 2)
                v.reciprocal(zi[:, two, :], ze[:, two, :]).then_inc(s["z_inv"], 1)

            def attend(b):
                dve.wait_ge(s["z_inv"], b + 1)
                if b >= 2:
                    wait_full(dve, "attnT", b - 2)
                for t in range(2 * b, 2 * b + 2):
                    v.tensor_tensor(at[:, b % 2, t % 2, :].rearrange("p (g h d) -> p g h d", g=FB, d=HD),
                                    num_of(t)[:, :, 0:P].rearrange("p g (h d) -> p g h d", d=HD),
                                    zi[:, t, :].rearrange("p (g h) -> p g h", g=FB).unsqueeze(3)
                                    .to_broadcast([P, FB, HPB, HD]), ALU.mult).then_inc(read_of("num", t), 1)

            def add_attn(p):
                wait_full(dve, "out", p)
                dve.wait_ge(s["xb"], 2 * p + 2)
                v.tensor_tensor(xs[:, 2 * p:2 * p + 2, :], B("out", p)[:, :].rearrange("p (t d) -> p t d", t=2),
                                xs[:, 2 * p:2 * p + 2, :], ALU.add).then_inc(read_of("out", p), 1)

            def ln2(h):
                a, z = h * HT, (h + 1) * HT
                for t in range(a, z):
                    norm_stats(2, t)
                for t in range(a, z):
                    norm_aggr(2, t)

            def times_score(t):
                dve.wait_ge(s["aggr2"], t + 1)
                wait_read(dve, "score", t // 2)
                v.scalar_tensor_tensor(score[:, t, :], xs[:, t, :], mv[:, 1, t, 0:1], score[:, t, :],
                                       ALU.subtract, ALU.mult).then_inc(s["sx"], 1)

            def logits(t):
                dve.wait_ge(s["rstd2"], t + 1)
                dve.wait_ge(s["sx"], t + 1)
                dve.wait_ge(s["mbias"], 2)
                v.tensor_tensor_reduce(out=score[:, t, :], in0=score[:, t, :], in1=mbias[:, t, :],
                                       scale=rstd[:, 1, t:t + 1], scalar=HIGHEST, op0=ALU.add, op1=ALU.min,
                                       accum_out=low[:, t:t + 1]).then_inc(s["logit"], 1)

            def softmax(h):
                a, z = h * HT, (h + 1) * HT
                for c in range(a, z, 2):
                    dve.wait_ge(s["prob"], c + 2)
                    v.reciprocal(rsum[:, c:c + 2], row_sum[:, c:c + 2]).then_inc(s["rsum"], 2)
                for t in range(a, z):
                    dve.wait_ge(s["rsum"], t + 1)
                    v.scalar_tensor_tensor(xs[:, t, :], score[:, t, :], rsum[:, t:t + 1], xs[:, t, :],
                                           ALU.mult, ALU.add).then_inc(s["x2"], 1)

            def ln3_stats(h):
                a, z = h * HT, (h + 1) * HT
                for t in range(a, z):
                    dve.wait_ge(s["x2"], t + 1)
                    norm_stats(3, t)
                for t in range(a, z):
                    norm_aggr(3, t)

            def ln3(h):
                for t in range(h * HT, (h + 1) * HT):
                    normalise(3, t)

            def x3T_lo(h):
                for f in range(FB):
                    dve.wait_ge(s["xs_hi"], FB * h + f + 1)
                    v.scalar_tensor_tensor(xs3[:, 1, f, :], B("x3T", h, f)[:, :], vecs[:, V_SUG + f:V_SUG + f + 1],
                                           xs3[:, 0, f, :].bitcast(F32), ALU.mult, ALU.subtract)\
                        .then_inc(read_of("x3T", h, f), 1)

            def xh_lo(h):
                for f in range(FB):
                    dve.wait_ge(s["xh_hi"], FB * h + f + 1)
                    v.tensor_tensor(xh[:, 1, h, f, :], B("xh", h, f)[:, :], xh[:, 0, h, f, :].bitcast(F32),
                                    ALU.subtract).then_inc(read_of("xh", h, f), 1)

            def add_y(half):
                for h, o, piece, a, z in PIECES:
                    if h == half:
                        wait_full(dve, "y", h, o, piece)
                        v.scalar_tensor_tensor(x2T[:, h, o, a:z], B("y", h, o, piece)[:, a:z], vecs[:, V_WSD + o:V_WSD + o + 1],
                                               x2T[:, h, o, a:z], ALU.mult, ALU.add).then_inc(s["y"], 1)

            def wd_lo(n):
                dve.wait_ge(s["wd_hi"], WDP * (n + 1))
                for i in range(WDP):
                    j = WDP * n + i
                    ins = v.scalar_tensor_tensor(
                        wdh[:, 1, j, :], B("wd", n)[:, i * HID:(i + 1) * HID],
                        vecs[:, V_SUD + j:V_SUD + j + 1], wdh[:, 0, j, :].bitcast(F32),
                        ALU.mult, ALU.subtract)
                ins.then_inc(read_of("wd", n), 1)

            ln1_stats(0, HT // 2, "x0")
            ln1_stats(HT // 2, HT, "x0_rest")
            ln1(0)
            wq_lo()
            xnT_lo(0)
            ln1_stats(HT, TILES, "x1")
            dve.wait_ge(ld["vec"], 16)
            elu_q(0, 0)
            elu_q(0, 1)
            ln1(1)
            dve.wait_ge(ld["row"], 16)
            kv(0)
            kv(1)
            for t in range(2, HT):
                elu_k(t - 2)
                kv(t)
            elu_k(2)
            elu_k(3)
            xnT_lo(1)
            dve.wait_ge(ld["cst"], 16)
            diagonal(0)
            diagonal(1)
            z_inverse(0)
            attend(0)
            z_inverse(1)
            attend(1)
            elu_q(1, 0)
            elu_q(1, 1)
            ug_lo(0)
            kv(4)
            add_attn(0)
            add_attn(1)
            kv(5)
            ln2(0)
            times_score(0)
            times_score(1)
            kv(6)
            times_score(2)
            times_score(3)
            kv(7)
            logits(0)
            logits(1)
            logits(2)
            logits(3)
            diagonal(2)
            softmax(0)
            diagonal(3)
            z_inverse(2)
            attend(2)
            ln3_stats(0)
            z_inverse(3)
            attend(3)
            ln3(0)
            add_attn(2)
            x3T_lo(0)
            add_attn(3)
            xh_lo(0)
            for n in range(WDB):
                wd_lo(n)
            for h in range(HALVES):
                for j in range(JB):
                    n = JB * h + j
                    wait_read(dve, "gate", h, j)
                    wait_full(dve, "up", h, j)
                    v.scalar_tensor_tensor(sg[:, n % 2, :], B("up", h, j)[:, :], vecs[:, V_WSUG + j:V_WSUG + j + 1],
                                           sg[:, n % 2, :], ALU.mult, ALU.mult).then_inc(read_of("up", h, j), 1)
                    if n == 0:
                        ln2(1)
                        for t in range(HT, TILES):
                            times_score(t)
                    if n == 1:
                        for t in range(HT, TILES):
                            logits(t)
                    if n == 2:
                        softmax(1)
                    if n == 3:
                        ln3_stats(1)
                    if n == 4:
                        ln3(1)
                    if n in ASIDE and ASIDE[n][0] != "x2T":
                        {"x3T": x3T_lo, "xh": xh_lo}[ASIDE[n][0]](1)
                    if n == JB + LAG - 1:
                        add_y(0)
            n = HALVES * JB - 1
            dve.wait_ge(s["h_hi"], n + 1)
            h_slot_free(dve, n)
            v.tensor_tensor(hsp[:, 1, n % HR, :], sg[:, n % 2, :], hsp[:, 0, n % HR, :].bitcast(F32),
                            ALU.subtract).then_inc(s["h_last"], 1)
            add_y(1)

        @block.tensor
        def _(pe):
            mm = nc.tensor.matmul

            def take(*group):
                if turn_of[group]:
                    pe.wait_ge(read_of(*group), turn_of[group])
                return B(*group)

            def done(ins, *group):
                ins.then_inc(full[bank_of[group]], 1)

            def weights_product():
                dst = take("mx")
                done(mm(dst[0:CTX1, 0:CTX1], wx[:, CTX1:2 * CTX1], wx[:, 0:CTX1], start=True, stop=True), "mx")

            def project(c):
                dst = take("u", c)
                done(mm(dst[0:CTX1, :], mx[:, :], ctxT[:, c * 512:(c + 1) * 512], start=True, stop=True), "u", c)

            def scores(b):
                wait_read(pe, "u", b // BPH)
                dst = take("score", b)
                for i in range(2):
                    ins = mm(dst[:, i * SEQ:(i + 1) * SEQ], ctxT[:, b * SEQ + i * P:b * SEQ + (i + 1) * P],
                             ux[:, b * SEQ:(b + 1) * SEQ], start=True, stop=True)
                done(ins, "score", b)

            def turn(name, h, src):
                for f in range(FB):
                    dst = take(name, h, f)
                    for i in range(HT):
                        ins = nc.tensor.transpose(dst[:, i * P:(i + 1) * P], src[:, i, f * P:(f + 1) * P], ident)
                    done(ins, name, h, f)

            def norm1(h):
                pe.wait_ge(s["xn1"], HT * (h + 1))
                turn("xnT", h, xn)

            def q_proj(h, m):
                dst = take("q", h, m)
                for i, (k, a, b) in enumerate(PASSES):
                    if m == 0 and a:
                        pe.wait_ge(s["xnT_hi"], FB * h + k + 1)
                    if m == 0 and b:
                        wait_read(pe, "xnT", h, k)
                    ins = mm(dst[:, :], wqkv[:, a, k, m * P:(m + 1) * P], xs3[:, b, k, :],
                             start=(i == 0), stop=(i == len(PASSES) - 1))
                done(ins, "q", h, m)

            def kv_proj(t):
                dst = take("kv", t)
                for i, (k, a, b) in enumerate(KV_PASSES):
                    if t == 0 and a:
                        pe.wait_ge(s["wkv_lo"], 1)
                    ins = mm(dst[:, :], xs3[:, b, k, t % HT * P:(t % HT + 1) * P], wqkv[:, a, k, HID:3 * HID],
                             start=(i == 0), stop=(i == len(PASSES) - 1))
                done(ins, "kv", t)

            def state(b):
                pe.wait_ge(s["kp"], 2 * b + 2)
                wait_read(pe, "kv", 2 * b)
                wait_read(pe, "kv", 2 * b + 1)
                dst = take("state", b)
                for g in range(FB):
                    for i in range(2):
                        ins = mm(dst[:, g * VW:(g + 1) * VW], kp[:, (2 * b + i) % HT, g * P:(g + 1) * P], vx[:, (2 * b + i) % HT, g, :],
                                 start=(i == 0), stop=(i == 1))
                done(ins, "state", b)

            def attend(b):
                pe.wait_ge(s["q"], FB * (b // BPH) + FB)
                wait_read(pe, "state", b)
                for t in range(2 * b, 2 * b + 2):
                    dst = take("num", t)
                    for g in range(FB):
                        ins = mm(dst[:, g * SW:(g + 1) * SW], qT[:, g, t * P:(t + 1) * P], kvs[:, b, g, :],
                                 start=True, stop=True)
                    done(ins, "num", t)

            def attn_turn(b):
                for i in range(2):
                    wait_read(pe, "num", 2 * b + i)
                dst = take("attnT", b)
                for g in range(FB):
                    for i in range(2):
                        ins = nc.tensor.transpose(dst[:, g * SEQ + i * P:g * SEQ + (i + 1) * P],
                                                  at[:, b % 2, i, g * P:(g + 1) * P], ident)
                done(ins, "attnT", b)

            def o_proj(p):
                wait_read(pe, "attnT", p)
                dst = take("out", p)
                for i in range(2):
                    for k in range(FB):
                        ins = mm(dst[:, i * HID:(i + 1) * HID], qT[:, k, (2 * p + i) * P:(2 * p + i + 1) * P], wo[:, k, :],
                                 start=(k == 0), stop=(k == FB - 1))
                done(ins, "out", p)

            def w_down(n):
                pe.wait_ge(s["pre_lo"], n * WDP // (JB // 2) + 1)
                dst = take("wd", n)
                for part in range(2):
                    ins = mm(dst[:, :], had_d[:, :], dpre[:, part, WDP * n:WDP * (n + 1), :].rearrange("p n o -> p (n o)"),
                             start=(part == 0), stop=(part == 1))
                done(ins, "wd", n)

            def x2_turn(h):
                pe.wait_ge(s["x2"], HT * (h + 1))
                turn("x2T", h, xs[:, h * HT:(h + 1) * HT, :])

            def x3_turn(h):
                pe.wait_ge(s["xn3"], HT * (h + 1))
                turn("x3T", h, xn)

            def hadamard_x(h):
                for f in range(FB):
                    dst = take("xh", h, f)
                    for part in range(2):
                        for k in range(FB):
                            if f == 0 and part == 0:
                                pe.wait_ge(s["xs_hi"], FB * h + k + 1)
                            if f == 0 and part == 1:
                                wait_read(pe, "x3T", h, k)
                            ins = mm(dst[:, :], (had_m if f and k else had_u)[:, :], xs3[:, part, k, :],
                                     start=(k == 0 and part == 0), stop=(k == FB - 1 and part == 1))
                    done(ins, "xh", h, f)

            def ffn_up(h, j):
                for name, at in (("gate", INTER), ("up", 0)):
                    dst = take(name, h, j)
                    for i, (k, a, b) in enumerate(PASSES):
                        if j == 0 and name == "gate" and a:
                            pe.wait_ge(s["xh_hi"], FB * h + k + 1)
                        if j == 0 and name == "gate" and b:
                            wait_read(pe, "xh", h, k)
                        ins = mm(dst[:, :], wug[:, a, k, at + j * P:at + (j + 1) * P], xh[:, b, h, k, :],
                                 start=(i == 0), stop=(i == len(PASSES) - 1))
                    done(ins, name, h, j)

            def down_product(h, j, o, a, b, piece, start=False, stop=False):
                c, d = {(ph, po, i): (c, d) for ph, po, i, c, d in PIECES}[h, o, piece]
                return mm(B("y", h, o, piece)[:, c:d], wdh[:, a, j, o * P:(o + 1) * P],
                          hsp[:, b, (JB * h + j) % HR, c:d], start=start, stop=stop)

            def pieces(h, o):
                return [i for ph, po, i, _, _ in PIECES if (ph, po) == (h, o)]

            def ffn_down(h, j):
                n = JB * h + j
                pe.wait_ge(s["h_hi"], n + 1)
                if j == 0 and h:
                    take("y", h, FB - 1, 1)
                for o in range(FB):
                    if j == 0 and h:
                        pe.wait_ge(s["y"], o + 1)
                    for a in (1, 0):
                        for i in pieces(h, o):
                            down_product(h, j, o, a, 0, i, start=(j == 0 and a == 1))
                pe.wait_ge(s["h_lo"], n + 1)
                for o in range(FB):
                    for i in pieces(h, o):
                        ins = down_product(h, j, o, 0, 1, i, stop=(j == JB - 1))
                    if j == JB - 1:
                        done(ins, "y", h, o, 0)
                if j < JB - 1:
                    ins.then_inc(s["h_used"], 1)

            def ffn_down_last():
                h, first = HALVES - 1, JB - LAG
                for o, piece in [(o, i) for o in range(FB) for i in pieces(h, o)]:
                    for j in range(first, JB):
                        n = JB * h + j
                        for a, b in ((1, 0), (0, 0), (0, 1)):
                            if o == 0 and a:
                                pe.wait_ge(s["h_hi"], n + 1)
                            if o == 0 and b:
                                if j == JB - 1:
                                    pe.wait_ge(s["h_last"], 1)
                                else:
                                    pe.wait_ge(s["h_lo"], n + 1)
                            ins = down_product(h, j, o, a, b, piece, stop=(j == JB - 1 and b == 1))
                    done(ins, "y", h, o, piece)

            pe.wait_ge(s["junk_ready"], 1)
            for _ in range(WARM):
                mm(bank[BANKS - 1][:, :], junk[:, 0:P], junk[:, :], start=True, stop=True)
            pe.wait_ge(ld["wx"], 16)
            weights_product()
            for _ in range(WARM_MORE):
                mm(bank[BANKS - 1][:, :], junk[:, 0:P], junk[:, :], start=True, stop=True)
            pe.wait_ge(ld["ident"], 16)
            norm1(0)
            pe.wait_ge(ld["ctx"], 16)
            wait_read(pe, "mx")
            project(0)
            pe.wait_ge(s["wq_lo"], 1)
            q_proj(0, 0)
            q_proj(0, 1)
            pe.wait_ge(s["w_hi"], 2)
            for t in range(HT):
                kv_proj(t)
            norm1(1)
            project(1)
            pe.wait_ge(s["ones_ready"], 1)
            state(0)
            state(1)
            q_proj(1, 0)
            attend(0)
            attend(1)
            q_proj(1, 1)
            attn_turn(0)
            attn_turn(1)
            kv_proj(HT)
            pe.wait_ge(ld["wo"], 16)
            o_proj(0)
            o_proj(1)
            kv_proj(HT + 1)
            scores(0)
            scores(1)
            kv_proj(HT + 2)
            kv_proj(HT + 3)
            state(2)
            scores(2)
            pe.wait_ge(s["had_ready"], 3)
            w_down(0)
            scores(3)
            attend(2)
            state(3)
            attend(3)
            attn_turn(2)
            w_down(1)
            o_proj(2)
            attn_turn(3)
            x3_turn(0)
            o_proj(3)
            hadamard_x(0)
            w_down(2)
            w_down(3)
            pe.wait_ge(s["ug_lo_v"], 1)
            pe.wait_ge(s["ug_lo_p"], 1)
            for h in range(HALVES):
                for j in range(JB):
                    if h == 0 and j == JB // 2:
                        pe.wait_ge(s["ug_lo_p"], 3)
                    ffn_up(h, j)
                    n = JB * h + j
                    if n in ASIDE:
                        step, half = ASIDE[n]
                        {"x2T": x2_turn, "x3T": x3_turn, "xh": hadamard_x}[step](half)
                    if n == LAG:
                        for i in range(WDB):
                            wait_read(pe, "wd", i)
                    if n >= LAG:
                        ffn_down((n - LAG) // JB, (n - LAG) % JB)
            ffn_down_last()


def kernel(**inputs):
    import concourse.bacc as _bacc
    from concourse.bass_utils import run_bass_kernel_spmd as _run

    a = {k: np.asarray(v) for k, v in inputs.items()}

    def blocks(w):
        return w.reshape(-1, P, w.shape[-1]).transpose(1, 0, 2)

    def columns(w):
        return w.reshape(-1, P).T

    eye, ones = np.eye(P, dtype=np.float32), np.ones((HD, HD), np.float32)
    arrays = {
        "x": blocks(a["x"].reshape(TOK, HID)),
        "ctx_t": np.concatenate([a["ctx_512"].reshape(TOK, CTX).T, np.ones((1, TOK), np.float32)]),
        "w_qkv": blocks(np.concatenate([a["L0_attn_q_w"], a["L0_attn_k_w"], a["L0_attn_v_w"]]).T),
        "w_o": blocks(a["L0_attn_o_w"].T),
        "w_x": np.concatenate([a["L0_xattn_Wq"], a["L0_xattn_bq"][:, None],
                               a["L0_xattn_Wk"], a["L0_xattn_bk"][:, None]], 1),
        "w_ug": blocks(np.concatenate([a["L0_ffn_W_up"], a["L0_ffn_W_gate"]]).T),
        "w_d": blocks(a["L0_ffn_W_down"].T),
        "vec": np.concatenate([columns(a[n]) for n in ("L0_attn_q_b", "L0_ffn_SU_ug", "L0_ffn_SU_dp",
                                                       "L0_ffn_Wscale_ug", "L0_ffn_Wscale_dp")], 1),
        "row": np.concatenate([a[n] for n in ("L0_attn_k_b", "L0_attn_v_b", "L0_attn_o_b")]),
        "mask_ss": blocks(a["mask_SxS2_bk1"]),
        "mask_key": a["mask_BxS2_bf0"],
        "const": np.concatenate([eye, hadamard(P), np.tile(np.kron(np.eye(P // HD, dtype=np.float32), ones), (1, FB)),
                                 np.tile(np.kron(np.eye(P // HD, dtype=np.float32), ones[:, 0:1]), (1, FB))], 1),
    }
    nc = _bacc.Bacc("TRN2", target_bir_lowering=False, num_devices=1)
    sent, args = {}, []
    for name, arr in arrays.items():
        arr = np.ascontiguousarray(arr)
        sent[f"in_{name}"] = arr
        args.append(nc.dram_tensor(f"in_{name}", arr.shape, mybir.dt.from_np(arr.dtype), kind="ExternalInput").ap())
    args.append(nc.dram_tensor("out_0", (P, FB, TOK), F32, kind="ExternalOutput").ap())
    decoder_kernel(nc, *args)
    got = _run(nc, [sent], core_ids=[0]).results[0]["out_0"]
    return np.ascontiguousarray(got.transpose(2, 1, 0)).reshape(BATCH, SEQ, HID)
```
